# Optimizing a Trainium2 kernel written in Bass

```python
import numpy as np
import jax
import jax.numpy as jnp

def _softmax(x, axis=-1):
    return jax.nn.softmax(x, axis=axis)

def _gelu(x):
    return jax.nn.gelu(x, approximate=True)

def _silu(x):
    return jax.nn.silu(x)

def _sigmoid(x):
    return jax.nn.sigmoid(x)

def _layernorm(x, axis=-1, eps=1e-05):
    m = jnp.mean(x, axis=axis, keepdims=True)
    v = jnp.var(x, axis=axis, keepdims=True)
    return (x - m) / jnp.sqrt(v + eps)

def _scatter_add(tgt, idx, src, axis=0):
    return tgt.at[idx].add(src)

def _segment_sum(src, seg, n):
    return jax.ops.segment_sum(src, seg, n)
kernel_name = 'mk_sandwich_d1_jaxref_r4_b7be8c'

def setup_inputs(seed: int=0):
    np.random.seed(seed)
    _w = jnp.asarray

    def _L0_attn_setup():
        import jax, jax.numpy as jnp
        import numpy as np
        B_SZ, SEQ, D_MODEL = (2, 512, 256)
        D_STATE, EXPAND = (16, 2)
        D_INNER = D_MODEL * EXPAND
        A_FLOOR = 0.0001
        RMS_EPS = float(np.finfo(np.float32).eps)

        def _rmsnorm(v, w):
            return v * jax.lax.rsqrt(jnp.mean(v * v, axis=-1, keepdims=True) + RMS_EPS) * w

        def _rope(v, cos_a, sin_a):
            ve, vo = (v[..., ::2], v[..., 1::2])
            re = ve * cos_a - vo * sin_a
            ro = ve * sin_a + vo * cos_a
            return jnp.stack([re, ro], axis=-1).reshape(v.shape)
        key = jax.random.key(seed)
        ks = jax.random.split(key, 6)
        x = jax.random.normal(ks[0], (B_SZ, SEQ, D_MODEL), dtype=jnp.float32)
        W_in = jax.random.normal(ks[1], (2 * D_INNER, D_MODEL), dtype=jnp.float32) * 0.02
        W_x = jax.random.normal(ks[2], (2 * D_STATE + 2, D_INNER), dtype=jnp.float32) * 0.02
        W_dt = jax.random.normal(ks[3], (D_INNER, 1), dtype=jnp.float32) * 0.1
        b_dt = jnp.zeros((D_INNER,), dtype=jnp.float32)
        A_log = jnp.broadcast_to(jnp.log(jnp.arange(1, D_STATE + 1, dtype=jnp.float32)), (D_INNER, D_STATE))
        B_bias = jnp.ones((D_STATE,), dtype=jnp.float32)
        C_bias = jnp.ones((D_STATE,), dtype=jnp.float32)
        B_norm_w = jnp.ones((D_STATE,), dtype=jnp.float32)
        C_norm_w = jnp.ones((D_STATE,), dtype=jnp.float32)
        rope_freqs = jax.random.normal(ks[4], (D_STATE // 2,), dtype=jnp.float32) * 0.01
        D = jnp.ones((D_INNER,), dtype=jnp.float32)
        W_out = jax.random.normal(ks[5], (D_MODEL, D_INNER), dtype=jnp.float32) * 0.02
        return {'x': x, 'W_in': W_in, 'W_x': W_x, 'W_dt': W_dt, 'b_dt': b_dt, 'A_log': A_log, 'B_bias': B_bias, 'C_bias': C_bias, 'B_norm_w': B_norm_w, 'C_norm_w': C_norm_w, 'rope_freqs': rope_freqs, 'D': D, 'W_out': W_out}
    _L0_attn_in = _L0_attn_setup()

    def _L0_ffn_setup():
        import jax, jax.numpy as jnp
        import numpy as np
        LN_EPS = 1e-05

        def layer_norm(x, g, b):
            mu = jnp.mean(x, axis=-1, keepdims=True)
            var = jnp.mean(jnp.square(x - mu), axis=-1, keepdims=True)
            return (x - mu) * jax.lax.rsqrt(var + LN_EPS) * g + b

        def ternary_quant(w):
            scale = 1.0 / jnp.clip(jnp.mean(jnp.abs(w)), 1e-05)
            wq = jnp.clip(jnp.round(w * scale), -1.0, 1.0) / scale
            return w + jax.lax.stop_gradient(wq - w)
        key = jax.random.key(seed)
        ks = jax.random.split(key, 3)
        dim, hidden = (256, 1024)
        B, S = (8, 256)
        x = jax.random.normal(ks[0], (B, S, dim), dtype=jnp.float32)
        w1 = jax.random.normal(ks[1], (hidden, dim), dtype=jnp.float32) * 0.02
        w2 = jax.random.normal(ks[2], (dim, hidden), dtype=jnp.float32) * 0.02
        return {'x': x, 'ln1_g': jnp.ones((dim,), jnp.float32), 'ln1_b': jnp.zeros((dim,), jnp.float32), 'w1': w1, 'b1': jnp.zeros((hidden,), jnp.float32), 'ln2_g': jnp.ones((hidden,), jnp.float32), 'ln2_b': jnp.zeros((hidden,), jnp.float32), 'w2': w2, 'b2': jnp.zeros((dim,), jnp.float32)}
    _L0_ffn_in = _L0_ffn_setup()
    _d = {'L0_attn_x': _L0_attn_in['x'], 'L0_attn_W_in': _L0_attn_in['W_in'], 'L0_attn_W_x': _L0_attn_in['W_x'], 'L0_attn_W_dt': _L0_attn_in['W_dt'], 'L0_attn_b_dt': _L0_attn_in['b_dt'], 'L0_attn_A_log': _L0_attn_in['A_log'], 'L0_attn_B_bias': _L0_attn_in['B_bias'], 'L0_attn_C_bias': _L0_attn_in['C_bias'], 'L0_attn_B_norm_w': _L0_attn_in['B_norm_w'], 'L0_attn_C_norm_w': _L0_attn_in['C_norm_w'], 'L0_attn_rope_freqs': _L0_attn_in['rope_freqs'], 'L0_attn_D': _L0_attn_in['D'], 'L0_attn_W_out': _L0_attn_in['W_out'], 'L0_ffn_ln1_g': _L0_ffn_in['ln1_g'], 'L0_ffn_ln1_b': _L0_ffn_in['ln1_b'], 'L0_ffn_w1': _L0_ffn_in['w1'], 'L0_ffn_b1': _L0_ffn_in['b1'], 'L0_ffn_ln2_g': _L0_ffn_in['ln2_g'], 'L0_ffn_ln2_b': _L0_ffn_in['ln2_b'], 'L0_ffn_w2': _L0_ffn_in['w2'], 'L0_ffn_b2': _L0_ffn_in['b2']}
    _x0 = _d['L0_attn_x']
    _d['L0_attn_x'] = jax.random.normal(jax.random.fold_in(jax.random.key(seed), 1), (2, 4096, 256), dtype=_x0.dtype)
    del _x0
    return _d

def reference(L0_attn_x, L0_attn_W_in, L0_attn_W_x, L0_attn_W_dt, L0_attn_b_dt, L0_attn_A_log, L0_attn_B_bias, L0_attn_C_bias, L0_attn_B_norm_w, L0_attn_C_norm_w, L0_attn_rope_freqs, L0_attn_D, L0_attn_W_out, L0_ffn_ln1_g, L0_ffn_ln1_b, L0_ffn_w1, L0_ffn_b1, L0_ffn_ln2_g, L0_ffn_ln2_b, L0_ffn_w2, L0_ffn_b2):

    def _L0_attn_ref(x, W_in, W_x, W_dt, b_dt, A_log, B_bias, C_bias, B_norm_w, C_norm_w, rope_freqs, D, W_out):
        import jax, jax.numpy as jnp
        import numpy as np
        B_SZ, SEQ, D_MODEL = (2, 512, 256)
        D_STATE, EXPAND = (16, 2)
        D_INNER = D_MODEL * EXPAND
        A_FLOOR = 0.0001
        RMS_EPS = float(np.finfo(np.float32).eps)

        def _rmsnorm(v, w):
            return v * jax.lax.rsqrt(jnp.mean(v * v, axis=-1, keepdims=True) + RMS_EPS) * w

        def _rope(v, cos_a, sin_a):
            ve, vo = (v[..., ::2], v[..., 1::2])
            re = ve * cos_a - vo * sin_a
            ro = ve * sin_a + vo * cos_a
            return jnp.stack([re, ro], axis=-1).reshape(v.shape)
        xz = jnp.einsum('bld,ed->ble', x, W_in)
        x_path, z = jnp.split(xz, 2, axis=-1)
        x_path = jax.nn.silu(x_path)
        ssm = jnp.einsum('ble,se->bls', x_path, W_x)
        B_raw = ssm[..., :D_STATE]
        C_raw = ssm[..., D_STATE:2 * D_STATE]
        dt_in = ssm[..., -2:-1]
        lam_in = ssm[..., -1:]
        Bn = _rmsnorm(B_raw + B_bias, B_norm_w)
        Cn = _rmsnorm(C_raw + C_bias, C_norm_w)
        dt = jax.nn.softplus(dt_in * W_dt[:, 0] + b_dt)
        lam = jax.nn.sigmoid(lam_in)
        freqs = jax.nn.softplus(rope_freqs)
        cum_dt = jnp.cumsum(jnp.mean(dt, axis=-1, keepdims=True), axis=1)
        angles = cum_dt * freqs
        cos_a, sin_a = (jnp.cos(angles), jnp.sin(angles))
        Br = _rope(Bn, cos_a, sin_a)
        Cr = _rope(Cn, cos_a, sin_a)
        A = jnp.minimum(-jnp.exp(A_log), -A_FLOOR)
        dA = jnp.exp(A[None, None] * dt[..., None])
        Bx = Br[:, :, None, :] * x_path[..., None]
        lam_e = lam[..., None]
        dt_e = dt[..., None]
        Bx_prev = jnp.concatenate([jnp.zeros_like(Bx[:, :1]), Bx[:, :-1]], axis=1)
        u = (1.0 - lam_e) * dt_e * dA * Bx_prev + lam_e * dt_e * Bx
        u = u.at[:, 0].set(dt_e[:, 0] * Bx[:, 0])
        dA_t = jnp.moveaxis(dA, 1, 0)
        u_t = jnp.moveaxis(u, 1, 0)
        C_t = jnp.moveaxis(Cr, 1, 0)

        def step(h, inp):
            dA_, u_, C_ = inp
            h = dA_ * h + u_
            y = jnp.sum(h * C_[:, None, :], axis=-1)
            return (h, y)
        h0 = jnp.zeros((x.shape[0], D_INNER, D_STATE), dtype=x.dtype)
        _, ys = jax.lax.scan(step, h0, (dA_t, u_t, C_t))
        y = jnp.moveaxis(ys, 0, 1)
        y = y + x_path * D
        y = y * jax.nn.silu(z)
        return jnp.einsum('ble,de->bld', y, W_out)

    def _L0_ffn_ref(x, ln1_g, ln1_b, w1, b1, ln2_g, ln2_b, w2, b2):
        import jax, jax.numpy as jnp
        import numpy as np
        LN_EPS = 1e-05

        def layer_norm(x, g, b):
            mu = jnp.mean(x, axis=-1, keepdims=True)
            var = jnp.mean(jnp.square(x - mu), axis=-1, keepdims=True)
            return (x - mu) * jax.lax.rsqrt(var + LN_EPS) * g + b

        def ternary_quant(w):
            scale = 1.0 / jnp.clip(jnp.mean(jnp.abs(w)), 1e-05)
            wq = jnp.clip(jnp.round(w * scale), -1.0, 1.0) / scale
            return w + jax.lax.stop_gradient(wq - w)
        h = layer_norm(x, ln1_g, ln1_b)
        h = jnp.einsum('bsd,hd->bsh', h, ternary_quant(w1)) + b1
        h = jax.nn.gelu(h, approximate=False)
        h = layer_norm(h, ln2_g, ln2_b)
        out = jnp.einsum('bsh,dh->bsd', h, ternary_quant(w2)) + b2
        return out
    x = L0_attn_x
    x = x + _layernorm(_L0_attn_ref(_layernorm(x, axis=-1), L0_attn_W_in, L0_attn_W_x, L0_attn_W_dt, L0_attn_b_dt, L0_attn_A_log, L0_attn_B_bias, L0_attn_C_bias, L0_attn_B_norm_w, L0_attn_C_norm_w, L0_attn_rope_freqs, L0_attn_D, L0_attn_W_out), axis=-1)
    x = x + _layernorm(_L0_ffn_ref(_layernorm(x, axis=-1), L0_ffn_ln1_g, L0_ffn_ln1_b, L0_ffn_w1, L0_ffn_b1, L0_ffn_ln2_g, L0_ffn_ln2_b, L0_ffn_w2, L0_ffn_b2), axis=-1)
    return x

_drawn_inputs = setup_inputs


def setup_inputs(seed=0):
    import zlib

    import numpy as np

    out = dict(_drawn_inputs(seed))
    spreads = {'L0_attn_b_dt': (0.0, 0.1),
     'L0_attn_B_bias': (1.0, 0.6),
     'L0_attn_C_bias': (1.0, 0.6),
     'L0_attn_B_norm_w': (1.0, 0.6),
     'L0_attn_C_norm_w': (1.0, 0.6),
     'L0_attn_D': (1.0, 0.6),
     'L0_ffn_ln1_g': (1.0, 0.2),
     'L0_ffn_ln1_b': (0.0, 0.1),
     'L0_ffn_b1': (0.0, 0.1),
     'L0_ffn_ln2_g': (1.0, 0.2),
     'L0_ffn_ln2_b': (0.0, 0.1),
     'L0_ffn_b2': (0.0, 0.1)}
    factors = {'L0_attn_W_x': 8.0, 'L0_attn_W_dt': 8.0, 'L0_attn_rope_freqs': 3.344}
    for name, (base, spread) in spreads.items():
        noise = np.random.default_rng([zlib.crc32(name.encode()), seed]).standard_normal(out[name].shape)
        drawn = base * np.exp(spread * noise) if base else spread * noise
        out[name] = jnp.asarray(drawn.astype(out[name].dtype))
    for name, factor in factors.items():
        out[name] = (out[name] * factor).astype(out[name].dtype)
    return out
```

```python
from contextlib import ExitStack

import numpy as np

import concourse.bass as bass
from concourse import mybir

F32 = mybir.dt.float32
ALU = mybir.AluOpType
ACT = mybir.ActivationFunctionType
AX = mybir.AxisListType.X

P = 128
TC = 512
NJ = TC // P
LN_EPS = 1e-5
RMS_EPS = float(np.finfo(np.float32).eps)
A_FLOOR = 1e-4
MAGIC = float(1.5 * 2 ** 23)
SCAN_TABLE = "natural_log_exp_and_others"
DVE_PAIRS = (1, 4, 6)


class Count:

    def __init__(self, sem):
        self.sem, self.value = sem, 0

    def up(self, n):
        self.value += n
        return (self.sem, self.value)


class Queue:

    def __init__(self):
        self.items, self.seen = [], {}

    def put(self, make, after=(), done=None, n=1):
        waits = []
        for t in after:
            if t is None:
                continue
            sem, value = t
            if self.seen.get(sem.name, 0) < value:
                self.seen[sem.name] = value
                waits.append(t)
        self.items.append((waits, make, done.sem if done else None, n))
        return done.up(n) if done else None

    def run(self, engine):
        for waits, make, sem, n in self.items:
            for s, value in waits:
                engine.wait_ge(s, value)
            ins = make(engine)
            if sem is not None:
                ins.then_inc(sem, n)


def block_kernel(nc, x, w_in, w_x, w_dt, b_dt, a_log, bc_bias, bc_norm, freqs, d_skip, w_out,
                 ln1_g, ln1_b, w1, b1, ln2_g, ln2_b, w2, b2, ident_in, tri_in, out, rows_dram):
    T, DM = x.shape
    KD = DM // P
    E = w_out.shape[1] * P
    KE = E // P
    NS = a_log.shape[2]
    NF = NS // 2
    HID = w1.shape[2]
    KH = HID // P
    NCH = T // TC
    PER_BATCH = NCH // 2
    HALF = TC // 2
    NROW = 2 * NS + 2
    LAM, NCB = 2 * NS, 2 * NS + 1
    DT_SLOTS = KE + 2
    G_PAIRS = 2
    C1 = 6.28125
    C2 = float(np.float32(int((2 * np.pi - C1) * 2 ** 20)) / 2 ** 20)
    C3 = float(2 * np.pi - C1 - C2)
    PI = 3.1415925

    with ExitStack() as ctx:
        total = [0]

        def sb(name, shape, dt=F32):
            total[0] += int(np.prod(shape[1:])) * 4
            return ctx.enter_context(nc.sbuf_tensor(name, shape, dt))

        def psum(name):
            return ctx.enter_context(nc.psum_tensor(name, [P, 512], F32))

        def count(name):
            return Count(ctx.enter_context(nc.semaphore(name)))

        ident = sb("ident", [P, P])
        tri = sb("tri", [P, P])
        ones = sb("ones", [P, P])
        w_in_sb = sb("w_in_sb", [P, KD, 2 * E])
        w_x_sb = sb("w_x_sb", [P, KE, 2 * NS + 2])
        w_out_sb = sb("w_out_sb", [P, KE, DM])
        w1_sb = sb("w1_sb", [P, KD, HID])
        w2_sb = sb("w2_sb", [P, KH, DM + 1])
        w_dt_sb = sb("w_dt_sb", [P, KE])
        b_dt_sb = sb("b_dt_sb", [P, KE])
        d_sb = sb("d_sb", [P, KE])
        a_sb = sb("a_sb", [P, KE, NS])
        bc_bias_sb = sb("bc_bias_sb", [P, NS, 2])
        bc_norm_sb = sb("bc_norm_sb", [P, NS, 2])
        freq_sb = sb("freq_sb", [P, NF])
        ln1_g_sb = sb("ln1_g_sb", [P, KD])
        ln1_b_sb = sb("ln1_b_sb", [P, KD])
        b1_sb = sb("b1_sb", [P, KH])
        ln2_g_sb = sb("ln2_g_sb", [P, KH])
        ln2_b_sb = sb("ln2_b_sb", [P, KH])
        sum_w2 = sb("sum_w2", [P, DM])
        bias_w2 = sb("bias_w2", [P, DM])
        ln_eps = sb("ln_eps", [P, 1])
        rms_eps = sb("rms_eps", [P, 1])
        inv_e = sb("inv_e", [P, 1])
        tern = sb("tern", [P, 4])
        stage = sb("stage", [P, NJ, DM])
        stats = sb("stats", [P, NJ, 6])
        mv = sb("mv", [P, NJ, 2])
        rstd = sb("rstd", [P, NJ])
        newton = sb("newton", [P, 2 * NJ])
        xn_t = sb("xn_t", [P, KD, TC])
        xp = sb("xp", [P, KE, TC])
        xp_last = sb("xp_last", [P, 2, KE])
        zs = sb("zs", [P, NJ, E])
        wide = sb("wide", [P, KE * TC])
        dt = sb("dt", [P, DT_SLOTS, TC])
        ssm = sb("ssm", [P, NJ, 2 * NS + 2])
        mdt = sb("mdt", [P, NJ])
        before = sb("before", [P, 2, NJ + 1])
        ang = sb("ang", [P, NJ, NF])
        turn = sb("turn", [P, NJ, 2, NF])
        rem = sb("rem", [P, NJ, 2, NF])
        sc = sb("sc", [P, NJ, 2, NF])
        bc = sb("bc", [P, NJ, NS, 2])
        bc_sq = sb("bc_sq", [P, NJ, NS, 2])
        ms = sb("ms", [P, NJ, 2])
        rms = sb("rms", [P, NJ, 2])
        rope_a = sb("rope_a", [P, NJ, NF, 2])
        rope_b = sb("rope_b", [P, NJ, NF, 2])
        lam_e = sb("lam_e", [P, NJ])
        rows_tm = sb("rows_tm", [P, NJ, P])
        lam_bc = sb("lam_bc", [P, TC])
        ncb_bc = sb("ncb_bc", [P, TC])
        bcb = sb("bcb", [P, NS, 2, TC])
        b_last = sb("b_last", [P, NS])
        lead = sb("lead", [P, TC])
        r_dt = sb("r_dt", [P, TC])
        late = sb("late", [P, 1])
        w = sb("w", [P, KE, TC])
        q = sb("q", [P, KE, TC])
        u = sb("u", [P, 2, 2, TC])
        g = sb("g", [P, G_PAIRS, 2, TC])
        state = sb("state", [P, KE, NS])
        gated = sb("gated", [P, NJ, P])
        yg = sb("yg", [P, KE, TC])
        x2 = sb("x2", [P, NJ, DM])
        h_t = sb("h_t", [P, KD, TC])
        sq = sb("sq", [P, 2, HALF])
        stats2 = sb("stats2", [P, NJ, 6])
        mv2 = sb("mv2", [P, NJ, 2])
        rstd2 = sb("rstd2", [P, NJ])
        newton2 = sb("newton2", [P, 2 * NJ])
        nmr = sb("nmr", [P, NJ])
        rows_sb = sq[:, :, :].rearrange("p a t -> p (a t)")
        hid = wide[:, :].rearrange("p (m t) -> p m t", m=KH)
        soft = wide[:, :].rearrange("p (m t) -> p m t", m=KE)

        psum_da = [psum(f"psum_da{i}") for i in range(2)]
        psum_g = psum("psum_g")
        psum_y = psum("psum_y")
        psum_f = [psum(f"psum_f{i}") for i in range(4)]

        names = ("c_const c_wprep c_actprep c_peprep c_xin c_xres c_stat c_rstd_a c_rstd c_norm c_xt c_xt_ev "
                 "c_proj c_silu c_xpl c_zproj c_zsilu c_dtp c_soft c_dt c_ssm c_mdt c_mdt_sb c_cum c_ang c_sin "
                 "c_bc c_ms c_lam_a c_rope c_rowt c_row_ev c_row_st c_wq c_da c_u c_scan c_state_p c_p_pool c_p_dve "
                 "c_y c_gate c_gt c_gt_ev c_out c_ln_a c_ln c_lnout c_x2 c_h c_ht c_ht_ev c_f1 c_gelu c_sq c_f2 "
                 "c_ffn c_res c_store c_stat2 c_rstd2_a c_rstd2 c_blast c_bstate c_lamld c_setup").split()
        k = {name: count(name) for name in names}
        c_piece = [count(f"c_piece{n}") for n in range(NS)]
        pe, act, dve, pool, sp = (Queue() for _ in range(5))

        free_banks = [(i, None) for i in range(4)]

        def take():
            assert free_banks, "no bank is free here"
            return free_banks.pop(0)

        def give(i, token):
            free_banks.append((i, token))

        loads = [(ident, ident_in), (tri, tri_in), (w_in_sb, w_in), (w_x_sb, w_x), (w_out_sb, w_out),
                 (w1_sb, w1), (w_dt_sb, w_dt), (b_dt_sb, b_dt), (d_sb, d_skip), (a_sb, a_log),
                 (ln1_g_sb, ln1_g), (ln1_b_sb, ln1_b), (b1_sb, b1), (ln2_g_sb, ln2_g), (ln2_b_sb, ln2_b)]
        def ap_of(t):
            return t[tuple(slice(None) for _ in t.shape)]
        for dst, src in loads:
            loaded = sp.put(lambda e, d=dst, s=src: e.dma_start(ap_of(d), s), done=k["c_const"], n=16)
        loaded = sp.put(lambda e: e.dma_start(w2_sb[:, :, 0:DM], w2), done=k["c_const"], n=16)
        for dst, src in ((bc_bias_sb[:, :, :], bc_bias), (bc_norm_sb[:, :, :], bc_norm)):
            loaded = sp.put(lambda e, d=dst, s=src: e.dma_start(d, s.partition_broadcast(P)), done=k["c_const"], n=16)
        loaded = sp.put(lambda e: e.dma_start(freq_sb[:, :], freqs.partition_broadcast(P)), done=k["c_const"], n=16)
        loaded = sp.put(lambda e: e.dma_start(bias_w2[:, :], b2.partition_broadcast(P)), done=k["c_const"], n=16)

        ones_set = dve.put(lambda e: e.memset(ones[:, :], 1.0), done=k["c_setup"])
        dve.put(lambda e: e.memset(ln_eps[:, :], LN_EPS), done=k["c_setup"])
        dve.put(lambda e: e.memset(rms_eps[:, :], RMS_EPS), done=k["c_setup"])
        dve.put(lambda e: e.memset(rows_tm[:, :, :], 0.0), done=k["c_setup"])
        consts_set = dve.put(lambda e: e.memset(inv_e[:, :], 1.0 / E), done=k["c_setup"])

        act.put(lambda e: e.preload_act_table_set(SCAN_TABLE))
        a_exp = act.put(lambda e: e.activation(a_sb[:, :, :], a_sb[:, :, :], ACT.Exp), (loaded,), k["c_actprep"])
        a_ready = dve.put(lambda e: e.tensor_scalar(a_sb[:, :, :], a_sb[:, :, :], -1.0, -A_FLOOR, ALU.mult, ALU.min),
                          (a_exp, loaded), k["c_wprep"])
        f0 = act.put(lambda e: e.activation(ang[:, 0, :], freq_sb[:, :], ACT.Abs), (), k["c_actprep"])
        f1 = act.put(lambda e: e.activation(ang[:, 1, :], ang[:, 0, :], ACT.Exp, scale=-1.0), (f0,), k["c_actprep"])
        f2 = act.put(lambda e: e.activation(ang[:, 2, :], ang[:, 1, :], ACT.Ln, bias=1.0), (f1,), k["c_actprep"])
        f3 = act.put(lambda e: e.activation(ang[:, 3, :], freq_sb[:, :], ACT.Relu), (), k["c_actprep"])
        freq_ready = dve.put(lambda e: e.tensor_tensor(freq_sb[:, :], ang[:, 2, :], ang[:, 3, :], ALU.add),
                             (f3,), k["c_wprep"])

        def ternary(wt, elements, n):
            last = freq_ready
            copy = wide[:, :].rearrange("p (a b) -> p a b", a=n)
            a = act.put(lambda e: e.activation(copy, wt, ACT.Abs, accum_out=tern[:, 0:1]), (last, k_last[0]),
                        k["c_actprep"])
            b = pe.put(lambda e: e.matmul(psum_f[0][:, 0:1], ones[:, :], tern[:, 0:1], start=True, stop=True),
                       (a, ones_set), k["c_peprep"])
            d = k["c_wprep"]
            t = dve.put(lambda e: e.tensor_scalar(tern[:, 1:2], psum_f[0][:, 0:1], 1.0 / elements, 1e-5, ALU.mult,
                                                  ALU.max), (b,), d)
            t = dve.put(lambda e: e.reciprocal(tern[:, 2:3], tern[:, 1:2]), (t,), d)
            t = dve.put(lambda e: e.reciprocal(tern[:, 3:4], tern[:, 2:3]), (t,), d)
            t = dve.put(lambda e: e.tensor_scalar(copy, wt, tern[:, 2:3], MAGIC, ALU.mult, ALU.add), (t, a), d)
            t = dve.put(lambda e: e.tensor_scalar(copy, copy, MAGIC, 1.0, ALU.subtract, ALU.min), (t,), d)
            t = dve.put(lambda e: e.tensor_scalar(copy, copy, -1.0, tern[:, 3:4], ALU.max, ALU.mult), (t,), d)
            t = dve.put(lambda e: e.tensor_tensor(copy, copy, wt, ALU.subtract), (t,), d)
            t = dve.put(lambda e: e.tensor_tensor(wt, wt, copy, ALU.add), (t,), d)
            k_last[0] = t
            return t

        k_last = [None]
        ternary(w1_sb[:, :, :], DM * HID, KD)
        w1_ready = k_last[0]
        w2_ready = ternary(w2_sb[:, :, 0:DM], DM * HID, KH)
        for m in range(KH):
            t = dve.put(lambda e, m=m: e.tensor_scalar(wide[:, m * P:(m + 1) * P], ones[:, :], ln2_b_sb[:, m:m + 1],
                                                       None, ALU.mult), (w2_ready,), k["c_wprep"])
        for m in range(KH):
            b = pe.put(lambda e, m=m: e.matmul(psum_f[1][:, 0:DM], wide[:, m * P:(m + 1) * P], w2_sb[:, m, 0:DM],
                                               start=m == 0, stop=m == KH - 1), (t,), k["c_peprep"])
        t = dve.put(lambda e: e.tensor_tensor(bias_w2[:, :], bias_w2[:, :], psum_f[1][:, 0:DM], ALU.add), (b,),
                    k["c_wprep"])
        for m in range(KH):
            t = dve.put(lambda e, m=m: e.tensor_scalar(w2_sb[:, m, 0:DM], w2_sb[:, m, 0:DM], ln2_g_sb[:, m:m + 1],
                                                       None, ALU.mult), (b, t), k["c_wprep"])
        t = dve.put(lambda e: e.memset(w2_sb[:, :, DM:DM + 1], 1.0 / HID), (), k["c_wprep"])
        for m in range(KH):
            b = pe.put(lambda e, m=m: e.matmul(psum_f[2][:, 0:DM], ones[:, :], w2_sb[:, m, 0:DM],
                                               start=m == 0, stop=m == KH - 1), (t,), k["c_peprep"])
        setup_done = dve.put(lambda e: e.tensor_copy(sum_w2[:, :], psum_f[2][:, 0:DM]), (b,), k["c_wprep"])
        for i in range(3):
            free_banks[i] = (i, setup_done)
        start_after = (loaded, setup_done, consts_set)

        S = [dict() for _ in range(NCH)]

        def first(c):
            return c % PER_BATCH == 0

        def rsqrt(var, y, tmp, eps, scale, after, c_a, c_d):
            n = y.shape[-1] if len(y.shape) == 2 else y.shape[-1] * y.shape[-2]
            t1, t2 = tmp
            a = act.put(lambda e: e.activation(t1, var, ACT.Ln, bias=eps[:, :], scale=scale), after, c_a)
            a = act.put(lambda e: e.activation(y, t1, ACT.Exp, scale=-0.5), (a,), c_a)
            eps_v = LN_EPS if eps is ln_eps else RMS_EPS

            def refine():
                d = dve.put(lambda e: e.tensor_tensor(t1, y, y, ALU.mult), (a,), c_d)
                d2 = dve.put(lambda e: e.tensor_scalar(t2, var, scale, eps_v, ALU.mult, ALU.add), (a,), c_d)
                d = dve.put(lambda e: e.tensor_tensor(t1, t1, t2, ALU.mult), (d2,), c_d)
                d = dve.put(lambda e: e.tensor_scalar(t1, t1, -0.5, 1.5, ALU.mult, ALU.add), (d,), c_d)
                return dve.put(lambda e: e.tensor_tensor(y, y, t1, ALU.mult), (d,), c_d)
            return refine

        def load_x(c):
            S[c]["x"] = sp.put(lambda e: e.dma_start(stage[:, :, :], x[c * TC:(c + 1) * TC, :].rearrange(
                "(j p) d -> p j d", p=P)), tuple(R.get("stage_free", ())), k["c_xin"], 16)

        def norm_stats(c):
            for j in range(NJ):
                t = dve.put(lambda e, j=j: e.bn_stats(stats[:, j, :], stage[:, j, :]), (S[c]["x"],), k["c_stat"])
            for j in range(NJ):
                t = dve.put(lambda e, j=j: e.bn_aggr(mv[:, j, :], stats[:, j, :]), (t,), k["c_stat"])
            S[c]["refine"] = rsqrt(mv[:, :, 1], rstd[:, :], (newton[:, 0:NJ], newton[:, NJ:]), ln_eps, 1.0,
                                   (t,) + start_after, k["c_rstd_a"], k["c_rstd"])

        def norm_x(c):
            r = S[c]["refine"]()
            for j in range(NJ):
                t = dve.put(lambda e, j=j: e.tensor_scalar(stage[:, j, :], stage[:, j, :], mv[:, j, 0:1],
                                                           rstd[:, j:j + 1], ALU.subtract, ALU.mult),
                            (r,), k["c_norm"])
            S[c]["xn"] = t

        def transpose_x(c):
            S[c]["xt"] = []
            for i in range(KD):
                b, fr = take()
                for j in range(NJ):
                    t = pe.put(lambda e, i=i, j=j, b=b: e.transpose(psum_f[b][:, j * P:(j + 1) * P],
                                                                   stage[:, j, i * P:(i + 1) * P], ident[:, :]),
                               (S[c]["xn"], fr, loaded), k["c_xt"])
                S[c]["xt"].append((b, t))
            R["stage_free"] = [t]

        def evict_xt(c):
            for i, (b, t) in enumerate(S[c]["xt"]):
                t = act.put(lambda e, i=i, b=b: e.copy(xn_t[:, i, :], psum_f[b][:, :]), (t, R.get("zproj")),
                            k["c_xt_ev"])
                give(b, t)
            S[c]["xnt"] = t

        def project_x(c):
            S[c]["proj"] = []
            for m in range(KE):
                b, fr = take()
                for i in range(KD):
                    t = pe.put(lambda e, i=i, m=m, b=b: e.matmul(psum_f[b][:, :], w_in_sb[:, i, m * P:(m + 1) * P],
                                                                xn_t[:, i, :], start=i == 0, stop=i == KD - 1),
                               (S[c]["xnt"], fr, loaded), k["c_proj"])
                S[c]["proj"].append((b, t))

        def silu_x(c):
            for m, (b, t) in enumerate(S[c]["proj"]):
                t = act.put(lambda e, m=m, b=b: e.activation(xp[:, m, :], psum_f[b][:, :], ACT.Silu),
                            (t, R.get("wq"), R.get("ssm_done")), k["c_silu"])
                give(b, t)
            act.put(lambda e: e.preload_act_table_set(SCAN_TABLE))
            S[c]["xp"] = t
            S[c]["xpl"] = dve.put(lambda e: e.tensor_copy(xp_last[:, c % 2, :], xp[:, :, TC - 1]), (t,), k["c_xpl"])

        def project_z(c):
            S[c]["zproj"] = []
            for j in range(NJ):
                b, fr = take()
                for i in range(KD):
                    t = pe.put(lambda e, i=i, j=j, b=b: e.matmul(psum_f[b][:, :], xn_t[:, i, j * P:(j + 1) * P],
                                                                w_in_sb[:, i, E:2 * E], start=i == 0,
                                                                stop=i == KD - 1),
                               (S[c]["xnt"], fr), k["c_zproj"])
                S[c]["zproj"].append((b, t))
            R["zproj"] = t

        def silu_z(c):
            for j, (b, t) in enumerate(S[c]["zproj"]):
                t = act.put(lambda e, j=j, b=b: e.activation(zs[:, j, :], psum_f[b][:, :], ACT.Silu),
                            (t, R.get("gate")), k["c_zsilu"])
                give(b, t)
            act.put(lambda e: e.preload_act_table_set(SCAN_TABLE))
            S[c]["zs"] = t

        def project_dt(c):
            b, fr = take()
            for m in range(KE):
                t = pe.put(lambda e, m=m, b=b: e.matmul(psum_f[b][:, :], w_x_sb[:, m, 2 * NS:2 * NS + 1]
                                                       .broadcast_to([P, P]), xp[:, m, :],
                                                       start=m == 0, stop=m == KE - 1),
                           (S[c]["xp"], fr), k["c_dtp"])
            S[c]["dtp"] = (b, t)
            b, fr = take()
            for j in range(NJ):
                for m in range(KE):
                    t = pe.put(lambda e, j=j, m=m, b=b: e.matmul(
                        psum_f[b][:, j * NROW:(j + 1) * NROW], xp[:, m, j * P:(j + 1) * P], w_x_sb[:, m, :],
                        start=m == 0, stop=m == KE - 1), (fr,), k["c_ssm"])
            R["ssm_done"] = t
            S[c]["ssm"] = (b, t)

        def slot(c, m):
            return (KE * c + m) % DT_SLOTS

        def softplus_dt(c):
            b, t = S[c]["dtp"]
            ca = k["c_soft"]
            for m in range(KE):
                a = act.put(lambda e, m=m: e.activation(soft[:, m, :], psum_f[b][:, :], ACT.Abs,
                                                        scale=w_dt_sb[:, m:m + 1], bias=b_dt_sb[:, m:m + 1]),
                            (t, R.get("hid_free")), ca)
            a = act.put(lambda e: e.activation(soft, soft, ACT.Exp, scale=-1.0), (a,), ca)
            a = act.put(lambda e: e.activation(soft, soft, ACT.Ln, bias=1.0), (a,), ca)
            for m in range(KE):
                a = act.put(lambda e, m=m: e.activation(dt[:, slot(c, m), :], psum_f[b][:, :], ACT.Relu,
                                                        scale=w_dt_sb[:, m:m + 1], bias=b_dt_sb[:, m:m + 1]),
                            (t, R.get("wq"), R.get("mdt_pe")), ca)
            give(b, a)
            S[c]["soft"] = a

        def add_dt(c):
            for m in range(KE):
                t = dve.put(lambda e, m=m: e.tensor_tensor(dt[:, slot(c, m), :], dt[:, slot(c, m), :], soft[:, m, :],
                                                           ALU.add), (S[c]["soft"],), k["c_dt"])
            S[c]["dt"] = t
            R["soft_free"] = t

        def mean_dt(c):
            b, _ = S[c]["ssm"]
            at = NJ * NROW
            for j in range(NJ):
                for m in range(KE):
                    t = pe.put(lambda e, j=j, m=m: e.matmul(psum_f[b][:, at + j:at + j + 1],
                                                            dt[:, slot(c, m), j * P:(j + 1) * P], inv_e[:, :],
                                                            start=m == 0, stop=m == KE - 1),
                               (S[c]["dt"], S[c]["ssm_sb"]), k["c_mdt"])
            R["mdt_pe"] = t
            S[c]["mdt"] = t

        def sums_dt(c):
            b, _ = S[c]["ssm"]
            at = NJ * NROW
            now, old = before[:, c % 2, :], before[:, 1 - c % 2, :]
            cd = k["c_mdt_sb"]
            if first(c):
                d = dve.put(lambda e: e.memset(now[:, 0:1], 0.0), (R.get("cum"),), cd)
            else:
                d = dve.put(lambda e: e.tensor_copy(now[:, 0:1], old[:, NJ:NJ + 1]), (R.get("cum"),), cd)
            d = dve.put(lambda e: e.tensor_copy(mdt[:, :], psum_f[b][:, at:at + NJ]), (S[c]["mdt"],), cd)
            d = dve.put(lambda e: e.tensor_tensor_scan(now[:, 1:NJ + 1], ones[:, 0:NJ], mdt[:, :], now[:, 0:1],
                                                       ALU.mult, ALU.add), (d,), cd)
            pe.put(lambda e: e.matmul(psum_f[b][:, at + NJ:at + 2 * NJ], tri[:, :], mdt[:, :], start=True,
                                      stop=False), (d,))
            R["cum"] = S[c]["cum"] = pe.put(
                lambda e: e.matmul(psum_f[b][:, at + NJ:at + 2 * NJ], ones[:, :], now[:, 0:NJ], start=False,
                                   stop=True), (d,), k["c_cum"])

        def bc_norms(c):
            b, t = S[c]["ssm"]
            cd = k["c_bc"]
            d = S[c]["ssm_sb"] = dve.put(lambda e: e.tensor_copy(
                ssm[:, :, :], psum_f[b][:, 0:NJ * NROW].rearrange("p (j r) -> p j r", j=NJ)), (t, R.get("lam_a")), cd)
            bias = bc_bias_sb[:, :, :].rearrange("p n a -> p (n a)").unsqueeze(1).broadcast_to([P, NJ, 2 * NS])
            flat = bc[:, :, :, :].rearrange("p j n a -> p j (n a)")
            d = dve.put(lambda e: e.tensor_tensor(flat, ssm[:, :, 0:2 * NS], bias, ALU.add),
                        (d,), cd)
            d = dve.put(lambda e: e.tensor_tensor(bc_sq[:, :, :, :], bc[:, :, :, :], bc[:, :, :, :], ALU.mult),
                        (d,), cd)
            for a in range(2):
                d = dve.put(lambda e, a=a: e.tensor_reduce(ms[:, :, a], bc_sq[:, :, :, a], AX, ALU.add), (d,), cd)
            S[c]["ms"] = d
            R["lam_a"] = S[c]["lam_a"] = act.put(
                lambda e: e.activation(lam_e[:, :], ssm[:, :, 2 * NS + 1], ACT.Exp, scale=-1.0),
                (S[c]["ssm_sb"], R.get("lam_free")), k["c_lam_a"])
            S[c]["refine_bc"] = rsqrt(ms[:, :, :], rms[:, :, :],
                                      (rope_a[:, :, 0, :], rope_b[:, :, 0, :]), rms_eps, 1.0 / NS, (d,),
                                      k["c_lam_a"], k["c_bc"])

        def angles(c):
            b, _ = S[c]["ssm"]
            at = NJ * NROW
            cum = psum_f[b][:, at + NJ:at + 2 * NJ].unsqueeze(2).broadcast_to([P, NJ, NF])
            fr = freq_sb[:, :].unsqueeze(1).broadcast_to([P, NJ, NF])
            cd = k["c_ang"]
            d = dve.put(lambda e: e.tensor_tensor(ang[:, :, :], cum, fr, ALU.mult), (S[c]["cum"], R.get("sin")), cd)
            for a, off in ((0, 0.0), (1, 0.25)):
                d2 = dve.put(lambda e, a=a, off=off: e.tensor_scalar(turn[:, :, a, :], ang[:, :, :],
                                                                     float(1 / (2 * np.pi)), off, ALU.mult, ALU.add),
                             (d,), cd)
            d = dve.put(lambda e: e.tensor_scalar(turn[:, :, :, :], turn[:, :, :, :], MAGIC, MAGIC, ALU.add,
                                                  ALU.subtract), (d2,), cd)
            d = dve.put(lambda e: e.tensor_scalar(turn[:, :, 1, :], turn[:, :, 1, :], -0.25, None, ALU.add), (d,), cd)
            for a in range(2):
                d2 = dve.put(lambda e, a=a: e.scalar_tensor_tensor(out=rem[:, :, a, :], in0=turn[:, :, a, :],
                                                                   scalar=-C1, in1=ang[:, :, :], op0=ALU.mult,
                                                                   op1=ALU.add), (d,), cd)
            flat_t = turn[:, :, :, :].rearrange("p j a f -> p (j a f)")
            flat_r = rem[:, :, :, :].rearrange("p j a f -> p (j a f)")
            for part in (C2, C3):
                d2 = dve.put(lambda e, part=part: e.scalar_tensor_tensor(out=flat_r, in0=flat_t, scalar=-part,
                                                                         in1=flat_r, op0=ALU.mult, op1=ALU.add),
                             (d2,), cd)
            S[c]["ang"] = dve.put(lambda e: e.tensor_scalar(flat_r, flat_r, -PI, PI, ALU.max, ALU.min), (d2,), cd)

        def sines(c):
            R["sin"] = S[c]["sin"] = act.put(lambda e: e.activation(sc[:, :, :, :], rem[:, :, :, :], ACT.Sin),
                                            (S[c]["ang"], R.get("rope")), k["c_sin"])
            act.put(lambda e: e.preload_act_table_set(SCAN_TABLE))

        def rope(c):
            cd = k["c_rope"]
            d = S[c]["refine_bc"]()
            for a in range(2):
                d = dve.put(lambda e, a=a: e.tensor_tensor(
                    bc[:, :, :, a], bc[:, :, :, a], rms[:, :, a:a + 1].broadcast_to([P, NJ, NS]), ALU.mult), (d,), cd)
            flat = bc[:, :, :, :].rearrange("p j n a -> p j (n a)")
            nw = bc_norm_sb[:, :, :].rearrange("p n a -> p (n a)").unsqueeze(1).broadcast_to([P, NJ, 2 * NS])
            d0 = dve.put(lambda e: e.tensor_tensor(flat, flat, nw, ALU.mult), (d,), cd)
            pairs = bc[:, :, :, :].rearrange("p j (f o) a -> p j f o a", o=2)
            even, odd = pairs[:, :, :, 0, :], pairs[:, :, :, 1, :]
            rows = rows_tm[:, :, 0:2 * NS].rearrange("p j (f o a) -> p j f o a", o=2, a=2)
            sin = sc[:, :, 0, :].unsqueeze(3).broadcast_to([P, NJ, NF, 2])
            cos = sc[:, :, 1, :].unsqueeze(3).broadcast_to([P, NJ, NF, 2])
            for which, (fa, fb, op) in enumerate(((cos, sin, ALU.subtract), (sin, cos, ALU.add))):
                dve.put(lambda e, fa=fa: e.tensor_tensor(rope_a[:, :, :, :], even, fa, ALU.mult),
                        (S[c]["sin"], d0, d if which else None), cd)
                d = dve.put(lambda e, fb=fb: e.tensor_tensor(rope_b[:, :, :, :], odd, fb, ALU.mult), (), cd)
                d = dve.put(lambda e, which=which, op=op: e.tensor_tensor(rows[:, :, :, which, :],
                                                                          rope_a[:, :, :, :], rope_b[:, :, :, :], op),
                            (d, R.get("rowt")), cd)
            made = rows_tm[:, :, 0:2 * NS].rearrange("p j (n a) -> p j n a", a=2)
            d = dve.put(lambda e: e.tensor_tensor(bc_sq[:, :, :, 0], made[:, :, :, 0], made[:, :, :, 1], ALU.mult),
                        (d,), cd)
            d = dve.put(lambda e: e.tensor_reduce(newton[:, 0:NJ], bc_sq[:, :, :, 0], AX, ALU.add), (d,), cd)
            d = dve.put(lambda e: e.tensor_scalar(rows_tm[:, :, NCB], newton[:, 0:NJ], -1.0, None, ALU.mult), (d,),
                        cd)
            d = dve.put(lambda e: e.tensor_scalar(lam_e[:, :], lam_e[:, :], 1.0, None, ALU.add), (S[c]["lam_a"],), cd)
            d = dve.put(lambda e: e.reciprocal(rows_tm[:, :, LAM], lam_e[:, :]), (d,), cd)
            if first(c):
                d = dve.put(lambda e: e.memset(rows_tm[0:1, 0, LAM:LAM + 1], 1.0), (d,), cd)
            R["rope"] = R["lam_free"] = S[c]["rope"] = d
            give(S[c]["ssm"][0], d)

        def transpose_rows(c):
            b, fr = take()
            for j in range(NJ):
                t = pe.put(lambda e, j=j, b=b: e.transpose(psum_f[b][:, j * P:(j + 1) * P], rows_tm[:, j, :],
                                                          ident[:, :]), (S[c]["rope"], fr), k["c_rowt"])
            R["rowt"] = t
            t = act.put(lambda e: e.copy(rows_sb[0:NROW, :], psum_f[b][0:NROW, :]), (t, R.get("row_st"), R.get(("sq", 1))),
                        k["c_row_ev"])
            give(b, t)
            R["row_st"] = S[c]["row_st"] = sp.put(lambda e: e.dma_start(rows_dram[c], rows_sb[0:NROW, :]), (t,),
                                                 k["c_row_st"], 16)

        def load_lam(c):
            for dst, row in ((lam_bc, LAM), (ncb_bc, NCB)):
                t = sp.put(lambda e, dst=dst, row=row: e.dma_start(dst[:, :], rows_dram[c][row, :].partition_broadcast(P)),
                           (S[c]["row_st"], R.get("wq")), k["c_lamld"], 16)
            S[c]["lam"] = t

        def load_piece(c, n):
            S[c][f"piece{n}"] = sp.put(
                lambda e: e.dma_start(bcb[:, n, :, :], rows_dram[c][2 * n:2 * n + 2, :].partition_broadcast(P)),
                (S[c]["row_st"], R.get(("u", n // 2)), R.get(("p", n // 2)), R.get("b_last")), c_piece[n], 16)

        def make_wq(c, m):
            cd = k["c_wq"]
            d_ = dt[:, slot(c, m), :]
            after = (S[c]["lam"], S[c]["dt"], S[c]["xp"], R.get("wq"))
            d = dve.put(lambda e: e.tensor_tensor(lead[:, :], lam_bc[:, :], d_, ALU.mult), after, cd)
            d = dve.put(lambda e: e.tensor_tensor(r_dt[:, :], d_, lead[:, :], ALU.subtract), (d,), cd)
            if not first(c):
                t = dve.put(lambda e: e.tensor_tensor(late[:, :], r_dt[:, 0:1], xp_last[:, (c - 1) % 2, m:m + 1],
                                                      ALU.mult), (d,), cd)
                S[c][f"state{m}"] = dve.put(lambda e: e.scalar_tensor_tensor(
                    out=state[:, m, :], in0=b_last[:, :], scalar=late[:, :], in1=state[:, m, :], op0=ALU.mult,
                    op1=ALU.add), (t, R["b_last"], R.get(("state_pool", m)), R.get(("state_dve", m))), cd)
            d = dve.put(lambda e: e.tensor_tensor(lead[:, 0:TC - 1], lead[:, 0:TC - 1], r_dt[:, 1:TC], ALU.add),
                        (d,), cd)
            d = dve.put(lambda e: e.tensor_tensor(w[:, m, :], lead[:, :], xp[:, m, :], ALU.mult),
                        (d, R.get(("w", m))), cd)
            S[c][f"w{m}"] = d
            dve.put(lambda e: e.memset(lead[:, TC - 1:TC], 0.0), (d,), cd)
            d = dve.put(lambda e: e.tensor_tensor(lead[:, 0:TC - 1], ncb_bc[:, 0:TC - 1], r_dt[:, 1:TC], ALU.mult),
                        (d,), cd)
            d = dve.put(lambda e: e.scalar_tensor_tensor(out=q[:, m, :], in0=lead[:, :], scalar=d_sb[:, m:m + 1],
                                                         in1=xp[:, m, :], op0=ALU.add, op1=ALU.mult),
                        (d, R.get(("q", m))), cd)
            R["wq"] = S[c][f"q{m}"] = d

        def make_u(c, m, i):
            ub = i % 2
            wb = w[:, m, :].unsqueeze(1).broadcast_to([P, 2, TC])
            t = pool.put(lambda e: e.tensor_tensor(u[:, ub, :, :], wb, bcb[:, 2 * i:2 * i + 2, 0, :], ALU.mult),
                         (S[c][f"w{m}"], S[c][f"piece{2 * i}"], S[c][f"piece{2 * i + 1}"], R.get(("u_free", ub))),
                         k["c_u"])
            R[("u", i)] = R[("w", m)] = S[c]["u", m, i] = t

        def scan_pair(c, m, i):
            n0, ub, gb = 2 * i, i % 2, i % G_PAIRS
            tu = S[c]["u", m, i]
            on_dve = i in DVE_PAIRS
            for a in range(2):
                n = n0 + a
                ta = act.put(lambda e, a=a, n=n: e.activation(psum_da[a][:, :], dt[:, slot(c, m), :], ACT.Exp,
                                                              scale=a_sb[:, m, n:n + 1]),
                             (S[c]["dt"], R.get(("da_free", a)), a_ready), k["c_da"])
                init = 0.0 if first(c) else state[:, m, n:n + 1]
                dst = psum_g[:, :] if on_dve else g[:, gb, a, :]
                ts = dve.put(lambda e, a=a, dst=dst, init=init: e.tensor_tensor_scan(
                    dst, psum_da[a][:, :], u[:, ub, a, :], init, ALU.mult, ALU.add),
                    (ta, tu, S[c].get(f"state{m}"), R.get(("g_free", gb)), R.get("psum_g") if on_dve else None),
                    k["c_scan"])
                R["da_free", a] = ts
                if on_dve:
                    dve.put(lambda e, n=n: e.tensor_copy(state[:, m, n:n + 1], psum_g[:, TC - 1:TC]), (ts,),
                            k["c_p_dve"])
                    tp = dve.put(lambda e, a=a, n=n: e.tensor_tensor(g[:, gb, a, :], psum_g[:, :],
                                                                    bcb[:, n, 1, :], ALU.mult), (ts,), k["c_p_dve"])
                    R["state_dve", m] = R["psum_g"] = tp
            R["u_free", ub] = ts
            nxt = (c, m, i + 1) if i + 1 < NS // 2 else (c, m + 1, 0) if m + 1 < KE else (c + 1, 0, 0)
            if nxt[0] < NCH:
                make_u(*nxt)
            if not on_dve:
                tc = pool.put(lambda e: e.tensor_copy(state[:, m, n0:n0 + 2], g[:, gb, :, TC - 1]), (ts,),
                              k["c_p_pool"])
                tp = pool.put(lambda e: e.tensor_tensor(g[:, gb, :, :], g[:, gb, :, :], bcb[:, n0:n0 + 2, 1, :],
                                                        ALU.mult), (tc,), k["c_p_pool"])
                R["state_pool", m] = tp
            R["p", i] = S[c]["p", m, i] = tp

        def add_up(c, m, i):
            gb = i % G_PAIRS
            if i == 0:
                for j in range(NJ):
                    t = pe.put(lambda e, j=j: e.matmul(psum_y[:, j * P:(j + 1) * P], q[:, m, j * P:(j + 1) * P],
                                                       ident[:, :], start=j == 0, stop=False, is_transpose=True,
                                                       skip_group_check=True),
                               (S[c][f"q{m}"], R.get("gate")), k["c_y"])
                R["q", m] = t
            for a in range(2):
                for j in range(NJ):
                    t = pe.put(lambda e, a=a, j=j: e.matmul(psum_y[:, j * P:(j + 1) * P],
                                                            g[:, gb, a, j * P:(j + 1) * P], ident[:, :],
                                                            start=False, stop=i == NS // 2 - 1, is_transpose=True,
                                                            skip_group_check=True), (S[c]["p", m, i],), k["c_y"])
            R["g_free", gb] = t
            S[c][f"y{m}"] = t

        def save_b_last(c):
            after = tuple(S[c][f"piece{n}"] for n in range(NS)) + (R.get("wq"),)
            R["b_last"] = dve.put(lambda e: e.tensor_copy(b_last[:, :], bcb[:, :, 0, TC - 1]), after, k["c_blast"])

        def gate(c, m):
            R["gate"] = S[c][f"gate{m}"] = dve.put(
                lambda e: e.tensor_tensor(gated[:, :, :], psum_y[:, :].rearrange("p (j e) -> p j e", j=NJ),
                                          zs[:, :, m * P:(m + 1) * P], ALU.mult),
                (S[c][f"y{m}"], S[c]["zs"], R.get("gt")), k["c_gate"])

        def transpose_gated(c, m):
            b, fr = take()
            for j in range(NJ):
                t = pe.put(lambda e, j=j, b=b: e.transpose(psum_f[b][:, j * P:(j + 1) * P], gated[:, j, :],
                                                          ident[:, :]), (S[c][f"gate{m}"], fr), k["c_gt"])
            R["gt"] = t
            t = act.put(lambda e: e.copy(yg[:, m, :], psum_f[b][:, :]), (t, R.get("outp")), k["c_gt_ev"])
            give(b, t)
            S[c]["yg"] = t

        def project_out(c):
            S[c]["res"] = sp.put(lambda e: e.dma_start(x2[:, :, :], x[c * TC:(c + 1) * TC, :].rearrange(
                "(j p) d -> p j d", p=P)), (R.get("x2_free"),), k["c_xres"], 16)
            S[c]["outp"] = []
            for h in range(NJ // 2):
                b, fr = take()
                for j2 in range(2):
                    j = 2 * h + j2
                    for m in range(KE):
                        t = pe.put(lambda e, j=j, j2=j2, m=m, b=b: e.matmul(
                            psum_f[b][:, j2 * DM:(j2 + 1) * DM], yg[:, m, j * P:(j + 1) * P], w_out_sb[:, m, :],
                            start=m == 0, stop=m == KE - 1), (S[c]["yg"], fr), k["c_out"])
                S[c]["outp"].append((b, t))
            R["outp"] = t

        def attn_stats(c):
            for j in range(NJ):
                b, t = S[c]["outp"][j // 2]
                d = dve.put(lambda e, j=j, b=b: e.bn_stats(stats2[:, j, :],
                                                          psum_f[b][:, (j % 2) * DM:(j % 2 + 1) * DM]), (t,),
                            k["c_stat2"])
            for j in range(NJ):
                d = dve.put(lambda e, j=j: e.bn_aggr(mv2[:, j, :], stats2[:, j, :]), (d,), k["c_stat2"])
            S[c]["refine2"] = rsqrt(mv2[:, :, 1], rstd2[:, :], (newton2[:, 0:NJ], newton2[:, NJ:]), ln_eps, 1.0,
                                    (d,), k["c_rstd2_a"], k["c_rstd2"])

        def minus_mean_rstd(after):
            d = dve.put(lambda e: e.tensor_tensor(nmr[:, :], mv2[:, :, 0], rstd2[:, :], ALU.mult), after,
                        k["c_rstd2"])
            return dve.put(lambda e: e.tensor_scalar(nmr[:, :], nmr[:, :], -1.0, None, ALU.mult), (d,), k["c_rstd2"])

        def attn_norm(c):
            r = S[c]["refine2"]()
            r = minus_mean_rstd((r,))
            for j in range(NJ):
                b, _ = S[c]["outp"][j // 2]
                d = dve.put(lambda e, j=j, b=b: e.scalar_tensor_tensor(
                    out=x2[:, j, :], in0=psum_f[b][:, (j % 2) * DM:(j % 2 + 1) * DM], scalar=rstd2[:, j:j + 1],
                    in1=x2[:, j, :], op0=ALU.mult, op1=ALU.add), (r, S[c]["res"]), k["c_x2"])
            for h in range(NJ // 2):
                give(S[c]["outp"][h][0], d)
            for j in range(NJ):
                d = dve.put(lambda e, j=j: e.tensor_scalar(x2[:, j, :], x2[:, j, :], nmr[:, j:j + 1], None, ALU.add),
                            (d,), k["c_x2"])
            S[c]["x2"] = d

        def ffn_stats(c):
            d = S[c]["x2"]
            for j in range(NJ):
                d = dve.put(lambda e, j=j: e.bn_stats(stats2[:, j, :], x2[:, j, :]), (S[c]["x2"],), k["c_stat2"])
            for j in range(NJ):
                d = dve.put(lambda e, j=j: e.bn_aggr(mv2[:, j, :], stats2[:, j, :]), (d,), k["c_stat2"])
            S[c]["refine2"] = rsqrt(mv2[:, :, 1], rstd2[:, :], (newton2[:, 0:NJ], newton2[:, NJ:]), ln_eps, 1.0,
                                    (d,), k["c_rstd2_a"], k["c_rstd2"])

        def ffn_stats2(c):
            r = S[c]["refine2"]()
            cd = k["c_rstd2"]
            d = dve.put(lambda e: e.tensor_copy(nmr[:, :], rstd2[:, :]), (r,), cd)
            d = dve.put(lambda e: e.tensor_tensor(mv2[:, :, 1], mv2[:, :, 1], rstd2[:, :], ALU.mult), (d,), cd)
            d = dve.put(lambda e: e.tensor_tensor(mv2[:, :, 1], mv2[:, :, 1], rstd2[:, :], ALU.mult), (d,), cd)
            S[c]["refine2"] = rsqrt(mv2[:, :, 1], rstd2[:, :], (newton2[:, 0:NJ], newton2[:, NJ:]), ln_eps, 1.0,
                                    (d,), k["c_rstd2_a"], k["c_rstd2"])

        def ffn_norm(c):
            r = S[c]["refine2"]()
            r = dve.put(lambda e: e.tensor_tensor(rstd2[:, :], rstd2[:, :], nmr[:, :], ALU.mult), (r,), k["c_rstd2"])
            for j in range(NJ):
                d = dve.put(lambda e, j=j: e.tensor_scalar(stage[:, j, :], x2[:, j, :], mv2[:, j, 0:1],
                                                           rstd2[:, j:j + 1], ALU.subtract, ALU.mult),
                            (r,) + tuple(R["stage_free"]), k["c_h"])
            S[c]["h"] = d

        def transpose_h(c):
            S[c]["ht"] = []
            for i in range(KD):
                b, fr = take()
                for j in range(NJ):
                    t = pe.put(lambda e, i=i, j=j, b=b: e.transpose(psum_f[b][:, j * P:(j + 1) * P],
                                                                   stage[:, j, i * P:(i + 1) * P], ident[:, :]),
                               (S[c]["h"], fr), k["c_ht"])
                S[c]["ht"].append((b, t))
            S[c]["stage_read"] = t

        def evict_ht(c):
            for i, (b, t) in enumerate(S[c]["ht"]):
                t = act.put(lambda e, i=i, b=b: e.activation(h_t[:, i, :], psum_f[b][:, :], ACT.Identity,
                                                             scale=ln1_g_sb[:, i:i + 1], bias=ln1_b_sb[:, i:i + 1]),
                            (t, R.get("f1")), k["c_ht_ev"])
                give(b, t)
            S[c]["h_t"] = t

        def ffn_up(c, half):
            S[c][f"f1{half}"] = []
            for m in range(0, KH, 2):
                b, fr = take()
                for m2 in range(2):
                    for i in range(KD):
                        t = pe.put(lambda e, i=i, m=m, m2=m2, b=b: e.matmul(
                            psum_f[b][:, m2 * HALF:(m2 + 1) * HALF], w1_sb[:, i, (m + m2) * P:(m + m2 + 1) * P],
                            h_t[:, i, half * HALF:(half + 1) * HALF], start=i == 0, stop=i == KD - 1),
                            (S[c]["h_t"], fr), k["c_f1"])
                S[c][f"f1{half}"].append((b, t))
            R["f1"] = t

        def ffn_gelu(c, half):
            for m in range(KH):
                b, t = S[c][f"f1{half}"][m // 2]
                t = act.put(lambda e, m=m, b=b: e.activation(hid[:, m, :], psum_f[b][:, (m % 2) * HALF:(m % 2 + 1) * HALF],
                                                             ACT.Gelu, bias=b1_sb[:, m:m + 1]),
                            (t, R.get("hid_free"), R.get("soft_free")), k["c_gelu"])
                if m % 2:
                    give(b, t)
            act.put(lambda e: e.preload_act_table_set(SCAN_TABLE))
            S[c][f"gelu{half}"] = t

        def ffn_down(c, half):
            banks = [take() for _ in range(2)]
            for m in range(KH):
                ts = act.put(lambda e, m=m: e.activation(sq[:, m % 2, :], hid[:, m, :], ACT.Square),
                             (S[c][f"gelu{half}"], R.get(("sq", m % 2)), R.get("row_st")), k["c_sq"])
                for j in range(2):
                    b, fr = banks[j]
                    pe.put(lambda e, m=m, j=j, b=b: e.matmul(
                        psum_f[b][:, 0:DM + 1], hid[:, m, j * P:(j + 1) * P], w2_sb[:, m, :], start=m == 0,
                        stop=m == KH - 1, skip_group_check=True), (S[c][f"gelu{half}"], fr), k["c_f2"])
                    t = pe.put(lambda e, m=m, j=j, b=b: e.matmul(
                        psum_f[b][:, DM + 1:DM + 2], sq[:, m % 2, j * P:(j + 1) * P], w2_sb[:, m, DM:DM + 1],
                        start=False, stop=m == KH - 1, skip_group_check=True), (ts,), k["c_f2"])
                R[("sq", m % 2)] = t
            R["hid_free"] = t
            S[c][f"f2{half}"] = (banks, t)

        def ffn_fold(c, half):
            banks, t = S[c][f"f2{half}"]
            cd = k["c_ffn"]
            sl = slice(2 * half, 2 * half + 2)
            for j in range(2):
                b = banks[j][0]
                d = dve.put(lambda e, j=j, b=b: e.tensor_copy(mv2[:, 2 * half + j, :], psum_f[b][:, DM:DM + 2]),
                            (t,), cd)
            d = dve.put(lambda e: e.tensor_tensor(nmr[:, sl], mv2[:, sl, 0], mv2[:, sl, 0], ALU.mult), (d,), cd)
            d = dve.put(lambda e: e.tensor_tensor(mv2[:, sl, 1], mv2[:, sl, 1], nmr[:, sl], ALU.subtract), (d,), cd)
            d = dve.put(lambda e: e.tensor_scalar(mv2[:, sl, 1], mv2[:, sl, 1], 0.0, None, ALU.max), (d,), cd)
            d2 = dve.put(lambda e: e.tensor_scalar(nmr[:, sl], mv2[:, sl, 0], -1.0, None, ALU.mult), (d,), cd)
            S[c]["refine2"] = rsqrt(mv2[:, sl, 1], rstd2[:, sl], (newton2[:, 0:2], newton2[:, NJ:NJ + 2]), ln_eps,
                                    1.0, (d2,), k["c_rstd2_a"], k["c_rstd2"])

        def ffn_out(c, half):
            banks, _ = S[c][f"f2{half}"]
            cd = k["c_ffn"]
            r = S[c]["refine2"]()
            for j in range(2):
                b, jj = banks[j][0], 2 * half + j
                d = dve.put(lambda e, b=b, jj=jj: e.scalar_tensor_tensor(
                    out=stage[:, jj, :], in0=sum_w2[:, :], scalar=nmr[:, jj:jj + 1], in1=psum_f[b][:, 0:DM],
                    op0=ALU.mult, op1=ALU.add), (r, S[c]["stage_read"]), cd)
                give(b, d)
                d = dve.put(lambda e, jj=jj: e.scalar_tensor_tensor(
                    out=stage[:, jj, :], in0=stage[:, jj, :], scalar=rstd2[:, jj:jj + 1], in1=bias_w2[:, :],
                    op0=ALU.mult, op1=ALU.add), (d,), cd)
            S[c]["o"] = d

        def last_stats(c):
            for j in range(NJ):
                d = dve.put(lambda e, j=j: e.bn_stats(stats2[:, j, :], stage[:, j, :]), (S[c]["o"],), k["c_stat2"])
            for j in range(NJ):
                d = dve.put(lambda e, j=j: e.bn_aggr(mv2[:, j, :], stats2[:, j, :]), (d,), k["c_stat2"])
            S[c]["refine2"] = rsqrt(mv2[:, :, 1], rstd2[:, :], (newton2[:, 0:NJ], newton2[:, NJ:]), ln_eps, 1.0,
                                    (d,), k["c_rstd2_a"], k["c_rstd2"])

        def last_norm(c):
            r = S[c]["refine2"]()
            r = minus_mean_rstd((r,))
            for j in range(NJ):
                d = dve.put(lambda e, j=j: e.scalar_tensor_tensor(
                    out=x2[:, j, :], in0=stage[:, j, :], scalar=rstd2[:, j:j + 1], in1=x2[:, j, :], op0=ALU.mult,
                    op1=ALU.add), (r,), k["c_res"])
            R["stage_free"] = [d]
            for j in range(NJ):
                d = dve.put(lambda e, j=j: e.tensor_scalar(x2[:, j, :], x2[:, j, :], nmr[:, j:j + 1], None, ALU.add),
                            (d,), k["c_res"])
            R["x2_free"] = sp.put(lambda e: e.dma_start(out[c * TC:(c + 1) * TC, :].rearrange(
                "(j p) d -> p j d", p=P), x2[:, :, :]), (d,), k["c_store"], 16)

        R = {}

        SIDE = [
            (0, project_z, 0), (4, silu_z, 0),
            (1, lambda c: make_wq(c, 1), 0), (3, lambda c: make_wq(c, 2), 0), (5, lambda c: make_wq(c, 3), 0),
            (6, save_b_last, 0),
            (5, load_x, 1), (7, norm_stats, 1), (9, norm_x, 1), (10, transpose_x, 1), (12, evict_xt, 1),
            (13, project_x, 1), (17, silu_x, 1),
            (17, project_out, -1), (21, attn_stats, -1), (23, attn_norm, -1), (24, ffn_stats, -1),
            (25, ffn_stats2, -1), (27, ffn_norm, -1), (28, transpose_h, -1), (30, evict_ht, -1),
            (36, project_dt, 1), (38, softplus_dt, 1), (39, add_dt, 1), (40, bc_norms, 1), (40, mean_dt, 1),
            (41, sums_dt, 1), (42, angles, 1), (43, sines, 1), (44, rope, 1), (45, transpose_rows, 1),
            (46, load_lam, 1),
            (45, lambda c: ffn_up(c, 0), -1), (49, lambda c: ffn_gelu(c, 0), -1), (51, lambda c: ffn_down(c, 0), -1),
            (53, lambda c: ffn_fold(c, 0), -1), (54, lambda c: ffn_out(c, 0), -1),
            (55, lambda c: ffn_up(c, 1), -1), (59, lambda c: ffn_gelu(c, 1), -1), (60, lambda c: ffn_down(c, 1), -1),
            (62, lambda c: ffn_fold(c, 1), -1), (63, lambda c: ffn_out(c, 1), -1),
            (63, last_stats, -1), (63, last_norm, -1), (61, lambda c: make_wq(c, 0), 1),
        ]
        SIDE.sort(key=lambda s: s[0])

        def side(c, at, only=None):
            for pos, stage_of, which in SIDE:
                if pos == at and 0 <= c + which < NCH and (only is None or which == only):
                    stage_of(c + which)

        for at in range(KE * NS):
            side(-1, at, 1)
            if at == 46:
                for n in range(NS):
                    load_piece(0, n)
        make_u(0, 0, 0)
        for c in range(NCH):
            for m in range(KE):
                for i in range(NS // 2):
                    at = m * NS + 2 * i
                    scan_pair(c, m, i)
                    if i == 0 and m:
                        gate(c, m - 1)
                    add_up(c, m, i)
                    if i == 1 and m:
                        transpose_gated(c, m - 1)
                    side(c, at)
                    side(c, at + 1)
                    if m == KE - 1 and c + 1 < NCH:
                        load_piece(c + 1, 2 * i)
                        load_piece(c + 1, 2 * i + 1)
            gate(c, KE - 1)
            transpose_gated(c, KE - 1)
        for at in range(KE * NS):
            side(NCH, at, -1)
        sp.put(lambda e: None, (R["x2_free"],))

        with nc.Block() as block:
            @block.sync
            def _(e):
                sp.run(e)

            @block.tensor
            def _(e):
                pe.run(e)

            @block.scalar
            def _(e):
                act.run(e)

            @block.vector
            def _(e):
                dve.run(e)

            @block.gpsimd
            def _(e):
                pool.run(e)


def kernel(**inputs):
    import concourse.bacc as bacc
    from concourse.bass_utils import run_bass_kernel_spmd

    a = {n.removeprefix("L0_"): np.asarray(v) for n, v in inputs.items()}
    x = a["attn_x"]
    B, L, DM = x.shape
    E, NS = a["attn_A_log"].shape
    HID = a["ffn_w1"].shape[0]

    def tiles(m):
        return np.ascontiguousarray(m.reshape(-1, P, m.shape[-1]).transpose(1, 0, 2))

    def columns(v):
        return np.ascontiguousarray(v.reshape(-1, P).T)

    order = np.concatenate([np.arange(2 * NS).reshape(2, NS).T.ravel(), [2 * NS, 2 * NS + 1]])
    arrays = {
        "x": x.reshape(B * L, DM),
        "w_in": tiles(a["attn_W_in"].T),
        "w_x": tiles(a["attn_W_x"].T[:, order]),
        "w_dt": columns(a["attn_W_dt"][:, 0]),
        "b_dt": columns(a["attn_b_dt"]),
        "a_log": tiles(a["attn_A_log"]),
        "bc_bias": np.stack([a["attn_B_bias"], a["attn_C_bias"]], 1),
        "bc_norm": np.stack([a["attn_B_norm_w"], a["attn_C_norm_w"]], 1),
        "freqs": a["attn_rope_freqs"],
        "d_skip": columns(a["attn_D"]),
        "w_out": tiles(a["attn_W_out"].T),
        "ln1_g": columns(a["ffn_ln1_g"]),
        "ln1_b": columns(a["ffn_ln1_b"]),
        "w1": tiles(a["ffn_w1"].T),
        "b1": columns(a["ffn_b1"]),
        "ln2_g": columns(a["ffn_ln2_g"]),
        "ln2_b": columns(a["ffn_ln2_b"]),
        "w2": tiles(a["ffn_w2"].T),
        "b2": a["ffn_b2"],
        "ident_in": np.eye(P, dtype=np.float32),
        "tri_in": np.triu(np.ones((P, P), np.float32)),
    }
    nc = bacc.Bacc("TRN2", target_bir_lowering=False, num_devices=1)
    arrays = {n: np.ascontiguousarray(v) for n, v in arrays.items()}
    args = {n: nc.dram_tensor(n, v.shape, mybir.dt.from_np(v.dtype), kind="ExternalInput").ap()
            for n, v in arrays.items()}
    out = nc.dram_tensor("out", (B * L, DM), F32, kind="ExternalOutput").ap()
    rows = nc.dram_tensor("rows", (B * L // TC, 2 * NS + 2, TC), F32, kind="Internal").ap()
    block_kernel(nc, out=out, rows_dram=rows, **args)
    r = run_bass_kernel_spmd(nc, [arrays], core_ids=[0])
    return r.results[0]["out"].reshape(B, L, DM)
```

```python
from contextlib import ExitStack

import numpy as np

import concourse.bass as bass
from concourse import mybir

F32 = mybir.dt.float32
ALU = mybir.AluOpType
ACT = mybir.ActivationFunctionType
AX = mybir.AxisListType.X

P = 128
TC = 512
NJ = TC // P
LN_EPS = 1e-5
RMS_EPS = float(np.finfo(np.float32).eps)
A_FLOOR = 1e-4
MAGIC = float(1.5 * 2 ** 23)
SCAN_TABLE = "natural_log_exp_and_others"
DVE_PAIRS = (1, 4, 6)


class Count:

    def __init__(self, sem):
        self.sem, self.value = sem, 0

    def up(self, n):
        self.value += n
        return (self.sem, self.value)


class Queue:

    def __init__(self):
        self.items, self.seen = [], {}

    def put(self, make, after=(), done=None, n=1):
        waits = []
        for t in after:
            if t is None:
                continue
            sem, value = t
            if self.seen.get(sem.name, 0) < value:
                self.seen[sem.name] = value
                waits.append(t)
        self.items.append((waits, make, done.sem if done else None, n))
        return done.up(n) if done else None

    def run(self, engine):
        for waits, make, sem, n in self.items:
            for s, value in waits:
                engine.wait_ge(s, value)
            ins = make(engine)
            if sem is not None:
                ins.then_inc(sem, n)


def block_kernel(nc, x, w_in, w_x, w_dt, b_dt, a_log, bc_bias, bc_norm, freqs, d_skip, w_out,
                 ln1_g, ln1_b, w1, b1, ln2_g, ln2_b, w2, b2, ident_in, tri_in, out, rows_dram):
    T, DM = x.shape
    KD = DM // P
    E = w_out.shape[1] * P
    KE = E // P
    NS = a_log.shape[2]
    NF = NS // 2
    HID = w1.shape[2]
    KH = HID // P
    NCH = T // TC
    PER_BATCH = NCH // 2
    HALF = TC // 2
    NROW = 2 * NS + 2
    LAM, NCB = 2 * NS, 2 * NS + 1
    DT_SLOTS = KE + 2
    N_SLOTS = 9
    G_PAIRS, U_PAIRS = 3, 2
    C1 = 6.28125
    C2 = float(np.float32(int((2 * np.pi - C1) * 2 ** 20)) / 2 ** 20)
    C3 = float(2 * np.pi - C1 - C2)
    PI = 3.1415925

    with ExitStack() as ctx:
        total = [0]

        def sb(name, shape, dt=F32):
            total[0] += int(np.prod(shape[1:])) * 4
            return ctx.enter_context(nc.sbuf_tensor(name, shape, dt))

        def psum(name):
            return ctx.enter_context(nc.psum_tensor(name, [P, 512], F32))

        def count(name):
            return Count(ctx.enter_context(nc.semaphore(name)))

        ident = sb("ident", [P, P])
        tri = sb("tri", [P, P])
        ones = sb("ones", [P, P])
        w_in_sb = sb("w_in_sb", [P, KD, 2 * E])
        w_x_sb = sb("w_x_sb", [P, KE, 2 * NS + 2])
        w_out_sb = sb("w_out_sb", [P, KE, DM])
        w1_sb = sb("w1_sb", [P, KD, HID])
        w2_sb = sb("w2_sb", [P, KH, DM + 1])
        w_dt_sb = sb("w_dt_sb", [P, KE])
        b_dt_sb = sb("b_dt_sb", [P, KE])
        d_sb = sb("d_sb", [P, KE])
        a_sb = sb("a_sb", [P, KE, NS])
        bc_bias_sb = sb("bc_bias_sb", [P, NS, 2])
        bc_norm_sb = sb("bc_norm_sb", [P, NS, 2])
        freq_sb = sb("freq_sb", [P, NF])
        ln1_g_sb = sb("ln1_g_sb", [P, KD])
        ln1_b_sb = sb("ln1_b_sb", [P, KD])
        b1_sb = sb("b1_sb", [P, KH])
        ln2_g_sb = sb("ln2_g_sb", [P, KH])
        ln2_b_sb = sb("ln2_b_sb", [P, KH])
        sum_w2 = sb("sum_w2", [P, DM])
        bias_w2 = sb("bias_w2", [P, DM])
        ln_eps = sb("ln_eps", [P, 1])
        rms_eps = sb("rms_eps", [P, 1])
        inv_e = sb("inv_e", [P, 1])
        tern = sb("tern", [P, 4])
        stage = sb("stage", [P, NJ, DM])
        stats = sb("stats", [P, NJ, 6])
        mv = sb("mv", [P, NJ, 2])
        rstd = sb("rstd", [P, NJ])
        newton = sb("newton", [P, 2 * NJ])
        xn_t = sb("xn_t", [P, KD, TC])
        xp_last = sb("xp_last", [P, 2, KE])
        zs = sb("zs", [P, NJ, E])
        wide = sb("wide", [P, KE * TC])
        dt = sb("dt", [P, DT_SLOTS, TC])
        ssm = sb("ssm", [P, NJ, 2 * NS + 2])
        mdt = sb("mdt", [P, NJ])
        before = sb("before", [P, 2, NJ + 1])
        ang = sb("ang", [P, NJ, NF])
        turn = sb("turn", [P, NJ, 2, NF])
        rem = sb("rem", [P, NJ, 2, NF])
        sc = sb("sc", [P, NJ, 2, NF])
        bc = sb("bc", [P, NJ, NS, 2])
        bc_sq = sb("bc_sq", [P, NJ, NS, 2])
        ms = sb("ms", [P, NJ, 2])
        rms = sb("rms", [P, NJ, 2])
        rope_a = sb("rope_a", [P, NJ, NF, 2])
        rope_b = sb("rope_b", [P, NJ, NF, 2])
        lam_e = sb("lam_e", [P, NJ])
        lam_bc = sb("lam_bc", [P, TC])
        ncb_bc = sb("ncb_bc", [P, TC])
        bcb = sb("bcb", [P, NS, 2, TC])
        b_last = sb("b_last", [P, NS])
        lead = sb("lead", [P, TC])
        r_dt = sb("r_dt", [P, TC])
        late = sb("late", [P, 1])
        slots = sb("slots", [P, N_SLOTS, TC])
        u = sb("u", [P, U_PAIRS, 2, TC])
        g = sb("g", [P, G_PAIRS, 2, TC])
        state = sb("state", [P, KE, NS])
        gated = sb("gated", [P, NJ, P])
        rows_tm = gated
        yg = sb("yg", [P, KE, TC])
        x2 = sb("x2", [P, NJ, DM])
        h_t = sb("h_t", [P, KD, TC])
        sq = sb("sq", [P, 2, HALF])
        stats2 = sb("stats2", [P, NJ, 6])
        mv2 = sb("mv2", [P, NJ, 2])
        rstd2 = sb("rstd2", [P, NJ])
        newton2 = sb("newton2", [P, 2 * NJ])
        nmr = sb("nmr", [P, NJ])
        rows_sb = sq[:, :, :].rearrange("p a t -> p (a t)")
        hid = wide[:, :].rearrange("p (m t) -> p m t", m=KH)
        soft = wide[:, :].rearrange("p (m t) -> p m t", m=KE)

        psum_da = [psum(f"psum_da{i}") for i in range(2)]
        psum_g = psum("psum_g")
        psum_y = psum("psum_y")
        psum_f = [psum(f"psum_f{i}") for i in range(4)]

        names = ("c_const c_wprep c_actprep c_peprep c_xin c_xres c_stat c_rstd_a c_rstd c_norm c_xt c_xt_ev "
                 "c_proj c_silu c_xpl c_zproj c_zsilu c_dtp c_soft c_dt c_ssm c_mdt c_mdt_sb c_cum c_ang c_sin "
                 "c_bc c_ms c_lam_a c_rope c_rowt c_row_ev c_row_st c_wq c_da c_u c_scan c_state_p c_p_pool c_p_dve "
                 "c_y c_gate c_gt c_gt_ev c_out c_ln_a c_ln c_lnout c_x2 c_h c_ht c_ht_ev c_f1 c_up_ev c_gelu c_sq c_f2 "
                 "c_ffn c_res c_store c_stat2 c_rstd2_a c_rstd2 c_blast c_bstate c_lamld c_setup").split()
        k = {name: count(name) for name in names}
        c_piece = [count(f"c_piece{n}") for n in range(NS)]
        pe, act, dve, pool, sp = (Queue() for _ in range(5))

        free_banks = [(i, None) for i in range(4)]

        def take():
            assert free_banks, "no bank is free here"
            return free_banks.pop(0)

        def give(i, token):
            free_banks.append((i, token))

        free_slots = [(i, None) for i in range(N_SLOTS)]

        loads = [(ident, ident_in), (tri, tri_in), (w_in_sb, w_in), (w_x_sb, w_x), (w_out_sb, w_out),
                 (w1_sb, w1), (w_dt_sb, w_dt), (b_dt_sb, b_dt), (d_sb, d_skip), (a_sb, a_log),
                 (ln1_g_sb, ln1_g), (ln1_b_sb, ln1_b), (b1_sb, b1), (ln2_g_sb, ln2_g), (ln2_b_sb, ln2_b)]
        def ap_of(t):
            return t[tuple(slice(None) for _ in t.shape)]
        for dst, src in loads:
            loaded = sp.put(lambda e, d=dst, s=src: e.dma_start(ap_of(d), s), done=k["c_const"], n=16)
        loaded = sp.put(lambda e: e.dma_start(w2_sb[:, :, 0:DM], w2), done=k["c_const"], n=16)
        for dst, src in ((bc_bias_sb[:, :, :], bc_bias), (bc_norm_sb[:, :, :], bc_norm)):
            loaded = sp.put(lambda e, d=dst, s=src: e.dma_start(d, s.partition_broadcast(P)), done=k["c_const"], n=16)
        loaded = sp.put(lambda e: e.dma_start(freq_sb[:, :], freqs.partition_broadcast(P)), done=k["c_const"], n=16)
        loaded = sp.put(lambda e: e.dma_start(bias_w2[:, :], b2.partition_broadcast(P)), done=k["c_const"], n=16)

        ones_set = dve.put(lambda e: e.memset(ones[:, :], 1.0), done=k["c_setup"])
        dve.put(lambda e: e.memset(ln_eps[:, :], LN_EPS), done=k["c_setup"])
        dve.put(lambda e: e.memset(rms_eps[:, :], RMS_EPS), done=k["c_setup"])
        dve.put(lambda e: e.memset(rows_tm[:, :, :], 0.0), done=k["c_setup"])
        consts_set = dve.put(lambda e: e.memset(inv_e[:, :], 1.0 / E), done=k["c_setup"])

        act.put(lambda e: e.preload_act_table_set(SCAN_TABLE))
        a_exp = act.put(lambda e: e.activation(a_sb[:, :, :], a_sb[:, :, :], ACT.Exp), (loaded,), k["c_actprep"])
        a_ready = dve.put(lambda e: e.tensor_scalar(a_sb[:, :, :], a_sb[:, :, :], -1.0, -A_FLOOR, ALU.mult, ALU.min),
                          (a_exp, loaded), k["c_wprep"])
        f0 = act.put(lambda e: e.activation(ang[:, 0, :], freq_sb[:, :], ACT.Abs), (), k["c_actprep"])
        f1 = act.put(lambda e: e.activation(ang[:, 1, :], ang[:, 0, :], ACT.Exp, scale=-1.0), (f0,), k["c_actprep"])
        f2 = act.put(lambda e: e.activation(ang[:, 2, :], ang[:, 1, :], ACT.Ln, bias=1.0), (f1,), k["c_actprep"])
        f3 = act.put(lambda e: e.activation(ang[:, 3, :], freq_sb[:, :], ACT.Relu), (), k["c_actprep"])
        freq_ready = dve.put(lambda e: e.tensor_tensor(freq_sb[:, :], ang[:, 2, :], ang[:, 3, :], ALU.add),
                             (f3,), k["c_wprep"])

        def ternary(wt, elements, n):
            last = freq_ready
            copy = wide[:, :].rearrange("p (a b) -> p a b", a=n)
            a = act.put(lambda e: e.activation(copy, wt, ACT.Abs, accum_out=tern[:, 0:1]), (last, k_last[0]),
                        k["c_actprep"])
            b = pe.put(lambda e: e.matmul(psum_f[0][:, 0:1], ones[:, :], tern[:, 0:1], start=True, stop=True),
                       (a, ones_set), k["c_peprep"])
            d = k["c_wprep"]
            t = dve.put(lambda e: e.tensor_scalar(tern[:, 1:2], psum_f[0][:, 0:1], 1.0 / elements, 1e-5, ALU.mult,
                                                  ALU.max), (b,), d)
            t = dve.put(lambda e: e.reciprocal(tern[:, 2:3], tern[:, 1:2]), (t,), d)
            t = dve.put(lambda e: e.reciprocal(tern[:, 3:4], tern[:, 2:3]), (t,), d)
            t = dve.put(lambda e: e.tensor_scalar(copy, wt, tern[:, 2:3], MAGIC, ALU.mult, ALU.add), (t, a), d)
            t = dve.put(lambda e: e.tensor_scalar(copy, copy, MAGIC, 1.0, ALU.subtract, ALU.min), (t,), d)
            t = dve.put(lambda e: e.tensor_scalar(copy, copy, -1.0, tern[:, 3:4], ALU.max, ALU.mult), (t,), d)
            t = dve.put(lambda e: e.tensor_tensor(copy, copy, wt, ALU.subtract), (t,), d)
            t = dve.put(lambda e: e.tensor_tensor(wt, wt, copy, ALU.add), (t,), d)
            k_last[0] = t
            return t

        k_last = [None]
        ternary(w1_sb[:, :, :], DM * HID, KD)
        w1_ready = k_last[0]
        w2_ready = ternary(w2_sb[:, :, 0:DM], DM * HID, KH)
        for m in range(KH):
            t = dve.put(lambda e, m=m: e.tensor_scalar(wide[:, m * P:(m + 1) * P], ones[:, :], ln2_b_sb[:, m:m + 1],
                                                       None, ALU.mult), (w2_ready,), k["c_wprep"])
        for m in range(KH):
            b = pe.put(lambda e, m=m: e.matmul(psum_f[1][:, 0:DM], wide[:, m * P:(m + 1) * P], w2_sb[:, m, 0:DM],
                                               start=m == 0, stop=m == KH - 1), (t,), k["c_peprep"])
        t = dve.put(lambda e: e.tensor_tensor(bias_w2[:, :], bias_w2[:, :], psum_f[1][:, 0:DM], ALU.add), (b,),
                    k["c_wprep"])
        for m in range(KH):
            t = dve.put(lambda e, m=m: e.tensor_scalar(w2_sb[:, m, 0:DM], w2_sb[:, m, 0:DM], ln2_g_sb[:, m:m + 1],
                                                       None, ALU.mult), (b, t), k["c_wprep"])
        t = dve.put(lambda e: e.memset(w2_sb[:, :, DM:DM + 1], 1.0 / HID), (), k["c_wprep"])
        for m in range(KH):
            b = pe.put(lambda e, m=m: e.matmul(psum_f[2][:, 0:DM], ones[:, :], w2_sb[:, m, 0:DM],
                                               start=m == 0, stop=m == KH - 1), (t,), k["c_peprep"])
        setup_done = dve.put(lambda e: e.tensor_copy(sum_w2[:, :], psum_f[2][:, 0:DM]), (b,), k["c_wprep"])
        for i in range(3):
            free_banks[i] = (i, setup_done)
        start_after = (loaded, setup_done, consts_set)

        S = [dict() for _ in range(NCH)]

        def first(c):
            return c % PER_BATCH == 0

        def rsqrt(var, y, tmp, eps, scale, after, c_a, c_d):
            t1, t2 = tmp
            yield 1
            a = act.put(lambda e: e.activation(t1, var, ACT.Ln, bias=eps[:, :], scale=scale), after, c_a)
            a = act.put(lambda e: e.activation(y, t1, ACT.Exp, scale=-0.5), (a,), c_a)
            eps_v = LN_EPS if eps is ln_eps else RMS_EPS
            yield 1
            dve.put(lambda e: e.tensor_tensor(t1, y, y, ALU.mult), (a,), c_d)
            d = dve.put(lambda e: e.tensor_scalar(t2, var, scale, eps_v, ALU.mult, ALU.add), (a,), c_d)
            d = dve.put(lambda e: e.tensor_tensor(t1, t1, t2, ALU.mult), (d,), c_d)
            d = dve.put(lambda e: e.tensor_scalar(t1, t1, -0.5, 1.5, ALU.mult, ALU.add), (d,), c_d)
            return dve.put(lambda e: e.tensor_tensor(y, y, t1, ALU.mult), (d,), c_d)

        def load_x(c):
            S[c]["x"] = sp.put(lambda e: e.dma_start(stage[:, :, :], x[c * TC:(c + 1) * TC, :].rearrange(
                "(j p) d -> p j d", p=P)), tuple(R.get("stage_free", ())), k["c_xin"], 16)

        def norm_x(c):
            for j in range(NJ):
                t = dve.put(lambda e, j=j: e.bn_stats(stats[:, j, :], stage[:, j, :]), (S[c]["x"],), k["c_stat"])
            for j in range(NJ):
                t = dve.put(lambda e, j=j: e.bn_aggr(mv[:, j, :], stats[:, j, :]), (t,), k["c_stat"])
            r = yield from rsqrt(mv[:, :, 1], rstd[:, :], (newton[:, 0:NJ], newton[:, NJ:]), ln_eps, 1.0,
                                 (t,) + start_after, k["c_rstd_a"], k["c_rstd"])
            for j in range(NJ):
                t = dve.put(lambda e, j=j: e.tensor_scalar(stage[:, j, :], stage[:, j, :], mv[:, j, 0:1],
                                                           rstd[:, j:j + 1], ALU.subtract, ALU.mult),
                            (r,), k["c_norm"])
            S[c]["xn"] = t

        def transpose_x(c):
            S[c]["xt"] = []
            for i in range(KD):
                b, fr = take()
                for j in range(NJ):
                    t = pe.put(lambda e, i=i, j=j, b=b: e.transpose(psum_f[b][:, j * P:(j + 1) * P],
                                                                   stage[:, j, i * P:(i + 1) * P], ident[:, :]),
                               (S[c]["xn"], fr, loaded), k["c_xt"])
                S[c]["xt"].append((b, t))
                R["stage_free"] = [t]
                yield 1
            for i, (b, t) in enumerate(S[c]["xt"]):
                t = act.put(lambda e, i=i, b=b: e.copy(xn_t[:, i, :], psum_f[b][:, :]), (t, R.get("zproj")),
                            k["c_xt_ev"])
                give(b, t)
            S[c]["xnt"] = t

        def project_x(c):
            S[c]["proj"] = []
            for m in range(KE):
                b, fr = take()
                for i in range(KD):
                    t = pe.put(lambda e, i=i, m=m, b=b: e.matmul(psum_f[b][:, :], w_in_sb[:, i, m * P:(m + 1) * P],
                                                                xn_t[:, i, :], start=i == 0, stop=i == KD - 1),
                               (S[c]["xnt"], fr, loaded), k["c_proj"])
                S[c]["proj"].append((b, t))
                yield 1
            yield 1
            for m, (b, t) in enumerate(S[c]["proj"]):
                xs, free = free_slots.pop(0)
                S[c]["xs", m] = xs
                t = act.put(lambda e, b=b, xs=xs: e.activation(slots[:, xs, :], psum_f[b][:, :], ACT.Silu),
                            (t,) + (free or ()), k["c_silu"])
                give(b, t)
            act.put(lambda e: e.preload_act_table_set(SCAN_TABLE))
            S[c]["xp"] = t

        def project_z(c):
            S[c]["zproj"] = []
            for j in range(NJ):
                b, fr = take()
                for i in range(KD):
                    t = pe.put(lambda e, i=i, j=j, b=b: e.matmul(psum_f[b][:, :], xn_t[:, i, j * P:(j + 1) * P],
                                                                w_in_sb[:, i, E:2 * E], start=i == 0,
                                                                stop=i == KD - 1),
                               (S[c]["xnt"], fr), k["c_zproj"])
                S[c]["zproj"].append((b, t))
                yield 1
            R["zproj"] = t
            yield 1
            for j, (b, t) in enumerate(S[c]["zproj"]):
                t = act.put(lambda e, j=j, b=b: e.activation(zs[:, j, :], psum_f[b][:, :], ACT.Silu),
                            (t, R.get("gate")), k["c_zsilu"])
                give(b, t)
            act.put(lambda e: e.preload_act_table_set(SCAN_TABLE))
            S[c]["zs"] = t

        def project_dt(c):
            b, fr = take()
            for m in range(KE):
                t = pe.put(lambda e, m=m, b=b: e.matmul(psum_f[b][:, :], w_x_sb[:, m, 2 * NS:2 * NS + 1]
                                                       .broadcast_to([P, P]), slots[:, S[c]["xs", m], :],
                                                       start=m == 0, stop=m == KE - 1),
                           (S[c]["xp"], fr), k["c_dtp"])
            S[c]["dtp"] = (b, t)
            yield 1
            b, fr = take()
            for j in range(NJ):
                for m in range(KE):
                    t = pe.put(lambda e, j=j, m=m, b=b: e.matmul(
                        psum_f[b][:, j * NROW:(j + 1) * NROW], slots[:, S[c]["xs", m], j * P:(j + 1) * P], w_x_sb[:, m, :],
                        start=m == 0, stop=m == KE - 1), (fr,), k["c_ssm"])
            S[c]["ssm_pe"] = t
            S[c]["ssm"] = (b, t)

        def slot(c, m):
            return (KE * c + m) % DT_SLOTS

        def softplus_dt(c):
            b, t = S[c]["dtp"]
            ca = k["c_soft"]
            for m in range(KE):
                a = act.put(lambda e, m=m: e.activation(soft[:, m, :], psum_f[b][:, :], ACT.Abs,
                                                        scale=w_dt_sb[:, m:m + 1], bias=b_dt_sb[:, m:m + 1]),
                            (t, R.get("hid_free")), ca)
            a = act.put(lambda e: e.activation(soft, soft, ACT.Exp, scale=-1.0), (a,), ca)
            a = act.put(lambda e: e.activation(soft, soft, ACT.Ln, bias=1.0), (a,), ca)
            for m in range(KE):
                a = act.put(lambda e, m=m: e.activation(dt[:, slot(c, m), :], psum_f[b][:, :], ACT.Relu,
                                                        scale=w_dt_sb[:, m:m + 1], bias=b_dt_sb[:, m:m + 1]),
                            (t, R.get("wq"), R.get("mdt_pe")), ca)
            give(b, a)
            S[c]["soft"] = a
            yield 1
            for m in range(KE):
                t = dve.put(lambda e, m=m: e.tensor_tensor(dt[:, slot(c, m), :], dt[:, slot(c, m), :], soft[:, m, :],
                                                           ALU.add), (S[c]["soft"],), k["c_dt"])
            S[c]["dt"] = t
            R["soft_free"] = t

        def mean_dt(c):
            b, fr = S[c]["sums"] = take()
            at = 0
            for j in range(NJ):
                for m in range(KE):
                    t = pe.put(lambda e, j=j, m=m: e.matmul(psum_f[b][:, at + j:at + j + 1],
                                                            dt[:, slot(c, m), j * P:(j + 1) * P], inv_e[:, :],
                                                            start=m == 0, stop=m == KE - 1),
                               (S[c]["dt"], fr), k["c_mdt"])
            R["mdt_pe"] = t
            S[c]["mdt"] = t

        def sums_dt(c):
            b, _ = S[c]["sums"]
            at = 0
            now, old = before[:, c % 2, :], before[:, 1 - c % 2, :]
            cd = k["c_mdt_sb"]
            if first(c):
                d = dve.put(lambda e: e.memset(now[:, 0:1], 0.0), (R.get("cum"),), cd)
            else:
                d = dve.put(lambda e: e.tensor_copy(now[:, 0:1], old[:, NJ:NJ + 1]), (R.get("cum"),), cd)
            d = dve.put(lambda e: e.tensor_copy(mdt[:, :], psum_f[b][:, at:at + NJ]), (S[c]["mdt"],), cd)
            d = dve.put(lambda e: e.tensor_tensor_scan(now[:, 1:NJ + 1], ones[:, 0:NJ], mdt[:, :], now[:, 0:1],
                                                       ALU.mult, ALU.add), (d,), cd)
            pe.put(lambda e: e.matmul(psum_f[b][:, at + NJ:at + 2 * NJ], tri[:, :], mdt[:, :], start=True,
                                      stop=False), (d,))
            R["cum"] = S[c]["cum"] = pe.put(
                lambda e: e.matmul(psum_f[b][:, at + NJ:at + 2 * NJ], ones[:, :], now[:, 0:NJ], start=False,
                                   stop=True), (d,), k["c_cum"])

        def bc_norms(c):
            b, t = S[c]["ssm"]
            cd = k["c_bc"]
            d = S[c]["ssm_sb"] = dve.put(lambda e: e.tensor_copy(
                ssm[:, :, :], psum_f[b][:, 0:NJ * NROW].rearrange("p (j r) -> p j r", j=NJ)), (t, R.get("lam_a")), cd)
            give(b, d)
            bias = bc_bias_sb[:, :, :].rearrange("p n a -> p (n a)").unsqueeze(1).broadcast_to([P, NJ, 2 * NS])
            flat = bc[:, :, :, :].rearrange("p j n a -> p j (n a)")
            d = dve.put(lambda e: e.tensor_tensor(flat, ssm[:, :, 0:2 * NS], bias, ALU.add),
                        (d,), cd)
            d = dve.put(lambda e: e.tensor_tensor(bc_sq[:, :, :, :], bc[:, :, :, :], bc[:, :, :, :], ALU.mult),
                        (d,), cd)
            for a in range(2):
                d = dve.put(lambda e, a=a: e.tensor_reduce(ms[:, :, a], bc_sq[:, :, :, a], AX, ALU.add), (d,), cd)
            S[c]["ms"] = d
            yield 1
            R["lam_a"] = S[c]["lam_a"] = act.put(
                lambda e: e.activation(lam_e[:, :], ssm[:, :, 2 * NS + 1], ACT.Exp, scale=-1.0),
                (S[c]["ssm_sb"], R.get("lam_free")), k["c_lam_a"])
            S[c]["rms"] = yield from rsqrt(ms[:, :, :], rms[:, :, :],
                                           (rope_a[:, :, 0, :], rope_b[:, :, 0, :]), rms_eps, 1.0 / NS, (d,),
                                           k["c_lam_a"], k["c_bc"])

        def angles(c):
            b, _ = S[c]["sums"]
            at = 0
            cum = psum_f[b][:, at + NJ:at + 2 * NJ].unsqueeze(2).broadcast_to([P, NJ, NF])
            fr = freq_sb[:, :].unsqueeze(1).broadcast_to([P, NJ, NF])
            cd = k["c_ang"]
            d = dve.put(lambda e: e.tensor_tensor(ang[:, :, :], cum, fr, ALU.mult), (S[c]["cum"], R.get("sin")), cd)
            give(b, d)
            for a, off in ((0, 0.0), (1, 0.25)):
                d2 = dve.put(lambda e, a=a, off=off: e.tensor_scalar(turn[:, :, a, :], ang[:, :, :],
                                                                     float(1 / (2 * np.pi)), off, ALU.mult, ALU.add),
                             (d,), cd)
            d = dve.put(lambda e: e.tensor_scalar(turn[:, :, :, :], turn[:, :, :, :], MAGIC, MAGIC, ALU.add,
                                                  ALU.subtract), (d2,), cd)
            d = dve.put(lambda e: e.tensor_scalar(turn[:, :, 1, :], turn[:, :, 1, :], -0.25, None, ALU.add), (d,), cd)
            for a in range(2):
                d2 = dve.put(lambda e, a=a: e.scalar_tensor_tensor(out=rem[:, :, a, :], in0=turn[:, :, a, :],
                                                                   scalar=-C1, in1=ang[:, :, :], op0=ALU.mult,
                                                                   op1=ALU.add), (d,), cd)
            flat_t = turn[:, :, :, :].rearrange("p j a f -> p (j a f)")
            flat_r = rem[:, :, :, :].rearrange("p j a f -> p (j a f)")
            for part in (C2, C3):
                d2 = dve.put(lambda e, part=part: e.scalar_tensor_tensor(out=flat_r, in0=flat_t, scalar=-part,
                                                                         in1=flat_r, op0=ALU.mult, op1=ALU.add),
                             (d2,), cd)
            S[c]["ang"] = dve.put(lambda e: e.tensor_scalar(flat_r, flat_r, -PI, PI, ALU.max, ALU.min), (d2,), cd)

        def sines(c):
            R["sin"] = S[c]["sin"] = act.put(lambda e: e.activation(sc[:, :, :, :], rem[:, :, :, :], ACT.Sin),
                                            (S[c]["ang"], R.get("rope")), k["c_sin"])
            act.put(lambda e: e.preload_act_table_set(SCAN_TABLE))

        def rope(c):
            cd = k["c_rope"]
            d = S[c]["rms"]
            for a in range(2):
                d = dve.put(lambda e, a=a: e.tensor_tensor(
                    bc[:, :, :, a], bc[:, :, :, a], rms[:, :, a:a + 1].broadcast_to([P, NJ, NS]), ALU.mult), (d,), cd)
            flat = bc[:, :, :, :].rearrange("p j n a -> p j (n a)")
            nw = bc_norm_sb[:, :, :].rearrange("p n a -> p (n a)").unsqueeze(1).broadcast_to([P, NJ, 2 * NS])
            d0 = dve.put(lambda e: e.tensor_tensor(flat, flat, nw, ALU.mult), (d,), cd)
            pairs = bc[:, :, :, :].rearrange("p j (f o) a -> p j f o a", o=2)
            even, odd = pairs[:, :, :, 0, :], pairs[:, :, :, 1, :]
            rows = rows_tm[:, :, 0:2 * NS].rearrange("p j (f o a) -> p j f o a", o=2, a=2)
            sin = sc[:, :, 0, :].unsqueeze(3).broadcast_to([P, NJ, NF, 2])
            cos = sc[:, :, 1, :].unsqueeze(3).broadcast_to([P, NJ, NF, 2])
            for which, (fa, fb, op) in enumerate(((cos, sin, ALU.subtract), (sin, cos, ALU.add))):
                dve.put(lambda e, fa=fa: e.tensor_tensor(rope_a[:, :, :, :], even, fa, ALU.mult),
                        (S[c]["sin"], d0, d if which else None), cd)
                d = dve.put(lambda e, fb=fb: e.tensor_tensor(rope_b[:, :, :, :], odd, fb, ALU.mult), (), cd)
                d = dve.put(lambda e, which=which, op=op: e.tensor_tensor(rows[:, :, :, which, :],
                                                                          rope_a[:, :, :, :], rope_b[:, :, :, :], op),
                            (d, R.get("gt")), cd)
            made = rows_tm[:, :, 0:2 * NS].rearrange("p j (n a) -> p j n a", a=2)
            d = dve.put(lambda e: e.tensor_tensor(bc_sq[:, :, :, 0], made[:, :, :, 0], made[:, :, :, 1], ALU.mult),
                        (d,), cd)
            d = dve.put(lambda e: e.tensor_reduce(newton[:, 0:NJ], bc_sq[:, :, :, 0], AX, ALU.add), (d,), cd)
            d = dve.put(lambda e: e.tensor_scalar(rows_tm[:, :, NCB], newton[:, 0:NJ], -1.0, None, ALU.mult), (d,),
                        cd)
            d = dve.put(lambda e: e.tensor_scalar(lam_e[:, :], lam_e[:, :], 1.0, None, ALU.add), (S[c]["lam_a"],), cd)
            d = dve.put(lambda e: e.reciprocal(rows_tm[:, :, LAM], lam_e[:, :]), (d,), cd)
            if first(c):
                d = dve.put(lambda e: e.memset(rows_tm[0:1, 0, LAM:LAM + 1], 1.0), (d,), cd)
            R["rope"] = R["lam_free"] = S[c]["rope"] = d

        def transpose_rows(c):
            b, fr = take()
            for j in range(NJ):
                t = pe.put(lambda e, j=j, b=b: e.transpose(psum_f[b][:, j * P:(j + 1) * P], rows_tm[:, j, :],
                                                          ident[:, :]), (S[c]["rope"], fr), k["c_rowt"])
            R["gt"] = t
            yield 1
            t = act.put(lambda e: e.copy(rows_sb[0:NROW, :], psum_f[b][0:NROW, :]), (t, R.get("row_st"), R.get(("sq", 1))),
                        k["c_row_ev"])
            give(b, t)
            R["row_st"] = S[c]["row_st"] = sp.put(lambda e: e.dma_start(rows_dram[c], rows_sb[0:NROW, :]), (t,),
                                                 k["c_row_st"], 16)

        def load_lam(c):
            for dst, row in ((lam_bc, LAM), (ncb_bc, NCB)):
                t = sp.put(lambda e, dst=dst, row=row: e.dma_start(dst[:, :], rows_dram[c][row, :].partition_broadcast(P)),
                           (S[c]["row_st"], R.get("wq")), k["c_lamld"], 16)
            S[c]["lam"] = t

        def load_pieces(c):
            for i in range(NS // 2):
                load_piece(c, 2 * i)
                load_piece(c, 2 * i + 1)
                if c and i + 1 < NS // 2:
                    yield 2

        def load_piece(c, n):
            S[c][f"piece{n}"] = sp.put(
                lambda e: e.dma_start(bcb[:, n, :, :], rows_dram[c][2 * n:2 * n + 2, :].partition_broadcast(P)),
                (S[c]["row_st"], R.get(("u", n // 2)), R.get(("p", n // 2)), R.get("b_last")), c_piece[n], 16)

        def make_wq(c, m):
            cd = k["c_wq"]
            d_ = dt[:, slot(c, m), :]
            xs = S[c]["xs", m]
            (ws, w_free), (qs, q_free) = free_slots.pop(0), free_slots.pop(0)
            S[c]["ws", m], S[c]["qs", m] = ws, qs
            dve.put(lambda e: e.tensor_copy(xp_last[:, c % 2, m:m + 1], slots[:, xs, TC - 1:TC]),
                    (S[c]["xp"], R.get("wq")), cd)
            after = (S[c]["lam"], S[c]["dt"], S[c]["xp"], R.get("wq"))
            d = dve.put(lambda e: e.tensor_tensor(lead[:, :], lam_bc[:, :], d_, ALU.mult), after, cd)
            d = dve.put(lambda e: e.tensor_tensor(r_dt[:, :], d_, lead[:, :], ALU.subtract), (d,), cd)
            if not first(c):
                t = dve.put(lambda e: e.tensor_tensor(late[:, :], r_dt[:, 0:1], xp_last[:, (c - 1) % 2, m:m + 1],
                                                      ALU.mult), (d,), cd)
                S[c][f"state{m}"] = dve.put(lambda e: e.scalar_tensor_tensor(
                    out=state[:, m, :], in0=b_last[:, :], scalar=late[:, :], in1=state[:, m, :], op0=ALU.mult,
                    op1=ALU.add), (t, R["b_last"], R.get(("state_pool", m)), R.get(("state_dve", m))), cd)
            d = dve.put(lambda e: e.tensor_tensor(lead[:, 0:TC - 1], lead[:, 0:TC - 1], r_dt[:, 1:TC], ALU.add),
                        (d,), cd)
            yield 1
            d = dve.put(lambda e: e.tensor_tensor(slots[:, ws, :], lead[:, :], slots[:, xs, :], ALU.mult),
                        (d,) + (w_free or ()), cd)
            S[c][f"w{m}"] = d
            t = dve.put(lambda e: e.memset(lead[:, TC - 1:TC], 0.0), (d,), cd)
            d = dve.put(lambda e: e.tensor_tensor(lead[:, 0:TC - 1], ncb_bc[:, 0:TC - 1], r_dt[:, 1:TC], ALU.mult),
                        (t,), cd)
            d = dve.put(lambda e: e.scalar_tensor_tensor(out=slots[:, qs, :], in0=lead[:, :], scalar=d_sb[:, m:m + 1],
                                                         in1=slots[:, xs, :], op0=ALU.add, op1=ALU.mult),
                        (d,) + (q_free or ()), cd)
            R["wq"] = S[c][f"q{m}"] = d
            free_slots.append((xs, (d, S[c]["ssm_pe"])))

        made_u = [0]
        U_AHEAD, G_AHEAD = 1, 1

        def after_pair(c, m, i, n):
            at = (c * KE + m) * (NS // 2) + i + n
            return (at // (KE * NS // 2), at // (NS // 2) % KE, at % (NS // 2)) if at < NCH * KE * NS // 2 else None

        def pair_no(c, m, i):
            return (c * KE + m) * (NS // 2) + i

        def make_da(c, m, i):
            for a in range(2):
                S[c]["da", m, i, a] = act.put(lambda e, a=a: e.activation(
                    psum_da[a][:, :], dt[:, slot(c, m), :], ACT.Exp, scale=a_sb[:, m, 2 * i + a:2 * i + a + 1]),
                    (S[c]["dt"], R.get(("da_free", a)), a_ready), k["c_da"])

        def make_u(c, m, i):
            ub = made_u[0] % U_PAIRS
            made_u[0] += 1
            wb = slots[:, S[c]["ws", m], :].unsqueeze(1).broadcast_to([P, 2, TC])
            t = pool.put(lambda e: e.tensor_tensor(u[:, ub, :, :], wb, bcb[:, 2 * i:2 * i + 2, 0, :], ALU.mult),
                         (S[c][f"w{m}"], S[c][f"piece{2 * i}"], S[c][f"piece{2 * i + 1}"], R.get(("u_free", ub))),
                         k["c_u"])
            R[("u", i)] = S[c]["u", m, i] = t
            S[c]["ub", m, i] = ub
            if i == NS // 2 - 1:
                free_slots.append((S[c]["ws", m], (t,)))

        def scan_pair(c, m, i):
            n0, ub, gb = 2 * i, S[c]["ub", m, i], pair_no(c, m, i) % G_PAIRS
            tu = S[c]["u", m, i]
            on_dve = i in DVE_PAIRS
            for a in range(2):
                n = n0 + a
                ta = S[c]["da", m, i, a]
                init = 0.0 if first(c) else state[:, m, n:n + 1]
                dst = psum_g[:, :] if on_dve else g[:, gb, a, :]
                ts = dve.put(lambda e, a=a, dst=dst, init=init: e.tensor_tensor_scan(
                    dst, psum_da[a][:, :], u[:, ub, a, :], init, ALU.mult, ALU.add),
                    (ta, tu, S[c].get(f"state{m}"), R.get(("g_free", gb)), R.get("psum_g") if on_dve else None),
                    k["c_scan"])
                R["da_free", a] = ts
                if on_dve:
                    dve.put(lambda e, n=n: e.tensor_copy(state[:, m, n:n + 1], psum_g[:, TC - 1:TC]), (ts,),
                            k["c_p_dve"])
                    tp = dve.put(lambda e, a=a, n=n: e.tensor_tensor(g[:, gb, a, :], psum_g[:, :],
                                                                    bcb[:, n, 1, :], ALU.mult), (ts,), k["c_p_dve"])
                    R["state_dve", m] = R["psum_g"] = tp
            R["u_free", ub] = ts
            nxt = after_pair(c, m, i, 1)
            if nxt:
                make_da(*nxt)
            nxt = after_pair(c, m, i, U_AHEAD)
            if nxt:
                make_u(*nxt)
            if not on_dve:
                tc = pool.put(lambda e: e.tensor_copy(state[:, m, n0:n0 + 2], g[:, gb, :, TC - 1]), (ts,),
                              k["c_p_pool"])
                tp = pool.put(lambda e: e.tensor_tensor(g[:, gb, :, :], g[:, gb, :, :], bcb[:, n0:n0 + 2, 1, :],
                                                        ALU.mult), (tc,), k["c_p_pool"])
                R["state_pool", m] = tp
            R["p", i] = S[c]["p", m, i] = tp

        def add_up(c, m, i):
            gb = pair_no(c, m, i) % G_PAIRS
            if i == 0:
                for j in range(NJ):
                    t = pe.put(lambda e, j=j: e.matmul(psum_y[:, j * P:(j + 1) * P], slots[:, S[c]["qs", m], j * P:(j + 1) * P],
                                                       ident[:, :], start=j == 0, stop=False, is_transpose=True,
                                                       skip_group_check=True),
                               (S[c][f"q{m}"], R.get("gate")), k["c_y"])
                free_slots.append((S[c]["qs", m], (t,)))
            for a in range(2):
                for j in range(NJ):
                    t = pe.put(lambda e, a=a, j=j: e.matmul(psum_y[:, j * P:(j + 1) * P],
                                                            g[:, gb, a, j * P:(j + 1) * P], ident[:, :],
                                                            start=False, stop=i == NS // 2 - 1, is_transpose=True,
                                                            skip_group_check=True), (S[c]["p", m, i],), k["c_y"])
            R["g_free", gb] = t
            S[c][f"y{m}"] = t

        def save_b_last(c):
            after = tuple(S[c][f"piece{n}"] for n in range(NS)) + (R.get("wq"),)
            R["b_last"] = dve.put(lambda e: e.tensor_copy(b_last[:, :], bcb[:, :, 0, TC - 1]), after, k["c_blast"])

        def gate(c, m):
            R["gate"] = S[c][f"gate{m}"] = dve.put(
                lambda e: e.tensor_tensor(gated[:, :, :], psum_y[:, :].rearrange("p (j e) -> p j e", j=NJ),
                                          zs[:, :, m * P:(m + 1) * P], ALU.mult),
                (S[c][f"y{m}"], S[c]["zs"], R.get("gt")), k["c_gate"])

        def transpose_gated(c, m):
            b, fr = take()
            for j in range(NJ):
                t = pe.put(lambda e, j=j, b=b: e.transpose(psum_f[b][:, j * P:(j + 1) * P], gated[:, j, :],
                                                          ident[:, :]), (S[c][f"gate{m}"], fr), k["c_gt"])
            R["gt"] = t
            yield 2
            t = act.put(lambda e: e.copy(yg[:, m, :], psum_f[b][:, :]), (t, R.get("outp")), k["c_gt_ev"])
            give(b, t)
            S[c]["yg"] = t

        def load_residual(c):
            S[c]["res"] = sp.put(lambda e: e.dma_start(x2[:, :, :], x[c * TC:(c + 1) * TC, :].rearrange(
                "(j p) d -> p j d", p=P)), (R.get("x2_free"),), k["c_xres"], 16)

        def project_out(c):
            S[c]["outp"] = []
            for h in range(NJ // 2):
                b, fr = take()
                for j2 in range(2):
                    j = 2 * h + j2
                    for m in range(KE):
                        t = pe.put(lambda e, j=j, j2=j2, m=m, b=b: e.matmul(
                            psum_f[b][:, j2 * DM:(j2 + 1) * DM], yg[:, m, j * P:(j + 1) * P], w_out_sb[:, m, :],
                            start=m == 0, stop=m == KE - 1), (S[c]["yg"], fr), k["c_out"])
                    yield 1
                S[c]["outp"].append((b, t))
            R["outp"] = t

        def minus_mean_rstd(after):
            d = dve.put(lambda e: e.tensor_tensor(nmr[:, :], mv2[:, :, 0], rstd2[:, :], ALU.mult), after,
                        k["c_rstd2"])
            return dve.put(lambda e: e.tensor_scalar(nmr[:, :], nmr[:, :], -1.0, None, ALU.mult), (d,), k["c_rstd2"])

        def attn_norm(c):
            for j in range(NJ):
                b, t = S[c]["outp"][j // 2]
                d = dve.put(lambda e, j=j, b=b: e.bn_stats(stats2[:, j, :],
                                                          psum_f[b][:, (j % 2) * DM:(j % 2 + 1) * DM]), (t,),
                            k["c_stat2"])
            for j in range(NJ):
                d = dve.put(lambda e, j=j: e.bn_aggr(mv2[:, j, :], stats2[:, j, :]), (d,), k["c_stat2"])
            r = yield from rsqrt(mv2[:, :, 1], rstd2[:, :], (newton2[:, 0:NJ], newton2[:, NJ:]), ln_eps, 1.0,
                                    (d,), k["c_rstd2_a"], k["c_rstd2"])

            r = minus_mean_rstd((r,))
            for j in range(NJ):
                b, _ = S[c]["outp"][j // 2]
                d = dve.put(lambda e, j=j, b=b: e.scalar_tensor_tensor(
                    out=x2[:, j, :], in0=psum_f[b][:, (j % 2) * DM:(j % 2 + 1) * DM], scalar=rstd2[:, j:j + 1],
                    in1=x2[:, j, :], op0=ALU.mult, op1=ALU.add), (r, S[c]["res"]), k["c_x2"])
            for h in range(NJ // 2):
                give(S[c]["outp"][h][0], d)
            for j in range(NJ):
                d = dve.put(lambda e, j=j: e.tensor_scalar(x2[:, j, :], x2[:, j, :], nmr[:, j:j + 1], None, ALU.add),
                            (d,), k["c_x2"])
            S[c]["x2"] = d

        def ffn_norm(c):
            d = S[c]["x2"]
            for j in range(NJ):
                d = dve.put(lambda e, j=j: e.bn_stats(stats2[:, j, :], x2[:, j, :]), (S[c]["x2"],), k["c_stat2"])
            for j in range(NJ):
                d = dve.put(lambda e, j=j: e.bn_aggr(mv2[:, j, :], stats2[:, j, :]), (d,), k["c_stat2"])
            r = yield from rsqrt(mv2[:, :, 1], rstd2[:, :], (newton2[:, 0:NJ], newton2[:, NJ:]), ln_eps, 1.0,
                                    (d,), k["c_rstd2_a"], k["c_rstd2"])
            cd = k["c_rstd2"]
            d = dve.put(lambda e: e.tensor_copy(nmr[:, :], rstd2[:, :]), (r,), cd)
            d = dve.put(lambda e: e.tensor_tensor(mv2[:, :, 1], mv2[:, :, 1], rstd2[:, :], ALU.mult), (d,), cd)
            d = dve.put(lambda e: e.tensor_tensor(mv2[:, :, 1], mv2[:, :, 1], rstd2[:, :], ALU.mult), (d,), cd)
            r = yield from rsqrt(mv2[:, :, 1], rstd2[:, :], (newton2[:, 0:NJ], newton2[:, NJ:]), ln_eps, 1.0,
                                    (d,), k["c_rstd2_a"], k["c_rstd2"])
            r = dve.put(lambda e: e.tensor_tensor(rstd2[:, :], rstd2[:, :], nmr[:, :], ALU.mult), (r,), k["c_rstd2"])
            for j in range(NJ):
                d = dve.put(lambda e, j=j: e.tensor_scalar(stage[:, j, :], x2[:, j, :], mv2[:, j, 0:1],
                                                           rstd2[:, j:j + 1], ALU.subtract, ALU.mult),
                            (r,) + tuple(R["stage_free"]), k["c_h"])
            S[c]["h"] = d

        def transpose_h(c):
            S[c]["ht"] = []
            for i in range(KD):
                b, fr = take()
                for j in range(NJ):
                    t = pe.put(lambda e, i=i, j=j, b=b: e.transpose(psum_f[b][:, j * P:(j + 1) * P],
                                                                   stage[:, j, i * P:(i + 1) * P], ident[:, :]),
                               (S[c]["h"], fr), k["c_ht"])
                S[c]["ht"].append((b, t))
                yield 1
            S[c]["stage_read"] = t
            for i, (b, t) in enumerate(S[c]["ht"]):
                t = act.put(lambda e, i=i, b=b: e.activation(h_t[:, i, :], psum_f[b][:, :], ACT.Identity,
                                                             scale=ln1_g_sb[:, i:i + 1], bias=ln1_b_sb[:, i:i + 1]),
                            (t, R.get("f1")), k["c_ht_ev"])
                give(b, t)
            S[c]["h_t"] = t

        def ffn_up(c, half):
            for m in range(0, KH, 2):
                b, fr = take()
                for m2 in range(2):
                    for i in range(KD):
                        t = pe.put(lambda e, i=i, m=m, m2=m2, b=b: e.matmul(
                            psum_f[b][:, m2 * HALF:(m2 + 1) * HALF], w1_sb[:, i, (m + m2) * P:(m + m2 + 1) * P],
                            h_t[:, i, half * HALF:(half + 1) * HALF], start=i == 0, stop=i == KD - 1),
                            (S[c]["h_t"], fr), k["c_f1"])
                yield 2
                for m2 in range(2):
                    a = act.put(lambda e, m=m, m2=m2, b=b: e.activation(
                        hid[:, m + m2, :], psum_f[b][:, m2 * HALF:(m2 + 1) * HALF], ACT.Identity,
                        bias=b1_sb[:, m + m2:m + m2 + 1]),
                        (t, R.get("hid_free"), R.get("soft_free")), k["c_up_ev"])
                give(b, a)
            R["f1"] = t
            for part in range(2):
                a2 = act.put(lambda e, part=part: e.activation(hid[:, 4 * part:4 * part + 4, :],
                                                               hid[:, 4 * part:4 * part + 4, :], ACT.Gelu), (a,),
                             k["c_gelu"])
            act.put(lambda e: e.preload_act_table_set(SCAN_TABLE))
            S[c][f"gelu{half}"] = a2

        def ffn_down(c, half):
            banks = [take() for _ in range(2)]

            def square(m):
                return act.put(lambda e, m=m: e.activation(sq[:, m % 2, :], hid[:, m, :], ACT.Square),
                               (S[c][f"gelu{half}"], R.get(("sq", m % 2)), R.get("row_st")), k["c_sq"])

            nxt = square(0)
            yield 1
            for m in range(KH):
                ts, nxt = nxt, square(m + 1) if m + 1 < KH else None
                for j in range(2):
                    b, fr = banks[j]
                    pe.put(lambda e, m=m, j=j, b=b: e.matmul(
                        psum_f[b][:, 0:DM + 1], hid[:, m, j * P:(j + 1) * P], w2_sb[:, m, :], start=m == 0,
                        stop=m == KH - 1, skip_group_check=True), (S[c][f"gelu{half}"], fr), k["c_f2"])
                    t = pe.put(lambda e, m=m, j=j, b=b: e.matmul(
                        psum_f[b][:, DM + 1:DM + 2], sq[:, m % 2, j * P:(j + 1) * P], w2_sb[:, m, DM:DM + 1],
                        start=False, stop=m == KH - 1, skip_group_check=True), (ts,), k["c_f2"])
                R[("sq", m % 2)] = t
                yield 1
            R["hid_free"] = t
            cd = k["c_ffn"]
            sl = slice(2 * half, 2 * half + 2)
            for j in range(2):
                b = banks[j][0]
                d = dve.put(lambda e, j=j, b=b: e.tensor_copy(mv2[:, 2 * half + j, :], psum_f[b][:, DM:DM + 2]),
                            (t,), cd)
            d = dve.put(lambda e: e.tensor_tensor(nmr[:, sl], mv2[:, sl, 0], mv2[:, sl, 0], ALU.mult), (d,), cd)
            d = dve.put(lambda e: e.tensor_tensor(mv2[:, sl, 1], mv2[:, sl, 1], nmr[:, sl], ALU.subtract), (d,), cd)
            d = dve.put(lambda e: e.tensor_scalar(mv2[:, sl, 1], mv2[:, sl, 1], 0.0, None, ALU.max), (d,), cd)
            d2 = dve.put(lambda e: e.tensor_scalar(nmr[:, sl], mv2[:, sl, 0], -1.0, None, ALU.mult), (d,), cd)
            r = yield from rsqrt(mv2[:, sl, 1], rstd2[:, sl], (newton2[:, 0:2], newton2[:, NJ:NJ + 2]), ln_eps,
                                 1.0, (d2,), k["c_rstd2_a"], k["c_rstd2"])
            for j in range(2):
                b, jj = banks[j][0], 2 * half + j
                d = dve.put(lambda e, b=b, jj=jj: e.scalar_tensor_tensor(
                    out=stage[:, jj, :], in0=sum_w2[:, :], scalar=nmr[:, jj:jj + 1], in1=psum_f[b][:, 0:DM],
                    op0=ALU.mult, op1=ALU.add), (r, S[c]["stage_read"]), cd)
                give(b, d)
                d = dve.put(lambda e, jj=jj: e.scalar_tensor_tensor(
                    out=stage[:, jj, :], in0=stage[:, jj, :], scalar=rstd2[:, jj:jj + 1], in1=bias_w2[:, :],
                    op0=ALU.mult, op1=ALU.add), (d,), cd)
            S[c]["o"] = d

        def last_norm(c):
            for j in range(NJ):
                d = dve.put(lambda e, j=j: e.bn_stats(stats2[:, j, :], stage[:, j, :]), (S[c]["o"],), k["c_stat2"])
            for j in range(NJ):
                d = dve.put(lambda e, j=j: e.bn_aggr(mv2[:, j, :], stats2[:, j, :]), (d,), k["c_stat2"])
            r = yield from rsqrt(mv2[:, :, 1], rstd2[:, :], (newton2[:, 0:NJ], newton2[:, NJ:]), ln_eps, 1.0,
                                    (d,), k["c_rstd2_a"], k["c_rstd2"])
            r = minus_mean_rstd((r,))
            for j in range(NJ):
                d = dve.put(lambda e, j=j: e.scalar_tensor_tensor(
                    out=x2[:, j, :], in0=stage[:, j, :], scalar=rstd2[:, j:j + 1], in1=x2[:, j, :], op0=ALU.mult,
                    op1=ALU.add), (r,), k["c_res"])
            R["stage_free"] = [d]
            for j in range(NJ):
                d = dve.put(lambda e, j=j: e.tensor_scalar(x2[:, j, :], x2[:, j, :], nmr[:, j:j + 1], None, ALU.add),
                            (d,), k["c_res"])
            R["x2_free"] = sp.put(lambda e: e.dma_start(out[c * TC:(c + 1) * TC, :].rearrange(
                "(j p) d -> p j d", p=P), x2[:, :, :]), (d,), k["c_store"], 16)

        R = {}

        SIDE = [
            (1, lambda c: make_wq(c, 1), 0), (3, lambda c: make_wq(c, 2), 0), (5, lambda c: make_wq(c, 3), 0),
            (7, save_b_last, 0),
            (9, project_z, 0),
            (14, load_x, 1), (17, norm_x, 1), (21, transpose_x, 1), (24, project_x, 1),
            (14, load_residual, -1), (14, project_out, -1), (18, attn_norm, -1), (22, ffn_norm, -1),
            (30, transpose_h, -1),
            (33, project_dt, 1), (36, softplus_dt, 1), (36, bc_norms, 1), (38, mean_dt, 1), (39, sums_dt, 1),
            (40, angles, 1), (41, sines, 1), (42, rope, 1), (44, transpose_rows, 1), (46, load_lam, 1),
            (48, load_pieces, 1),
            (38, lambda c: ffn_up(c, 0), -1), (46, lambda c: ffn_down(c, 0), -1),
            (55, lambda c: ffn_up(c, 1), -1), (0, lambda c: ffn_down(c, 1), -2), (11, last_norm, -2),
            (60, lambda c: make_wq(c, 0), 1),
        ]
        going = []

        def side(c, at):
            now = c * KE * NS + at
            for pos, stage_of, which in SIDE:
                if pos == at and 0 <= c + which < NCH:
                    steps = stage_of(c + which)
                    if steps is not None:
                        going.append([now, steps])
            for g_ in list(going):
                if g_[0] <= now:
                    try:
                        g_[0] = now + next(g_[1])
                    except StopIteration:
                        going.remove(g_)

        for at in range(KE * NS):
            side(-1, at)
        make_da(0, 0, 0)
        make_u(0, 0, 0)
        late_pair = None
        for c in range(NCH + 2):
            for at in range(0, KE * NS, 2):
                m, i = at // NS, at % NS // 2
                if c < NCH:
                    scan_pair(c, m, i)
                if i == 1 and 0 < c * KE + m <= NCH * KE:
                    last = divmod(c * KE + m - 1, KE)
                    gate(*last)
                    going.append([c * KE * NS + at + 2, transpose_gated(*last)])
                side(c, at)
                side(c, at + 1)
                if late_pair:
                    add_up(*late_pair)
                late_pair = (c, m, i) if c < NCH else None
        sp.put(lambda e: None, (R["x2_free"],))

        with nc.Block() as block:
            @block.sync
            def _(e):
                sp.run(e)

            @block.tensor
            def _(e):
                pe.run(e)

            @block.scalar
            def _(e):
                act.run(e)

            @block.vector
            def _(e):
                dve.run(e)

            @block.gpsimd
            def _(e):
                pool.run(e)


def kernel(**inputs):
    import concourse.bacc as bacc
    from concourse.bass_utils import run_bass_kernel_spmd

    a = {n.removeprefix("L0_"): np.asarray(v) for n, v in inputs.items()}
    x = a["attn_x"]
    B, L, DM = x.shape
    E, NS = a["attn_A_log"].shape
    HID = a["ffn_w1"].shape[0]

    def tiles(m):
        return np.ascontiguousarray(m.reshape(-1, P, m.shape[-1]).transpose(1, 0, 2))

    def columns(v):
        return np.ascontiguousarray(v.reshape(-1, P).T)

    order = np.concatenate([np.arange(2 * NS).reshape(2, NS).T.ravel(), [2 * NS, 2 * NS + 1]])
    arrays = {
        "x": x.reshape(B * L, DM),
        "w_in": tiles(a["attn_W_in"].T),
        "w_x": tiles(a["attn_W_x"].T[:, order]),
        "w_dt": columns(a["attn_W_dt"][:, 0]),
        "b_dt": columns(a["attn_b_dt"]),
        "a_log": tiles(a["attn_A_log"]),
        "bc_bias": np.stack([a["attn_B_bias"], a["attn_C_bias"]], 1),
        "bc_norm": np.stack([a["attn_B_norm_w"], a["attn_C_norm_w"]], 1),
        "freqs": a["attn_rope_freqs"],
        "d_skip": columns(a["attn_D"]),
        "w_out": tiles(a["attn_W_out"].T),
        "ln1_g": columns(a["ffn_ln1_g"]),
        "ln1_b": columns(a["ffn_ln1_b"]),
        "w1": tiles(a["ffn_w1"].T),
        "b1": columns(a["ffn_b1"]),
        "ln2_g": columns(a["ffn_ln2_g"]),
        "ln2_b": columns(a["ffn_ln2_b"]),
        "w2": tiles(a["ffn_w2"].T),
        "b2": a["ffn_b2"],
        "ident_in": np.eye(P, dtype=np.float32),
        "tri_in": np.triu(np.ones((P, P), np.float32)),
    }
    nc = bacc.Bacc("TRN2", target_bir_lowering=False, num_devices=1)
    arrays = {n: np.ascontiguousarray(v) for n, v in arrays.items()}
    args = {n: nc.dram_tensor(n, v.shape, mybir.dt.from_np(v.dtype), kind="ExternalInput").ap()
            for n, v in arrays.items()}
    out = nc.dram_tensor("out", (B * L, DM), F32, kind="ExternalOutput").ap()
    rows = nc.dram_tensor("rows", (B * L // TC, 2 * NS + 2, TC), F32, kind="Internal").ap()
    block_kernel(nc, out=out, rows_dram=rows, **args)
    r = run_bass_kernel_spmd(nc, [arrays], core_ids=[0])
    return r.results[0]["out"].reshape(B, L, DM)
```

```python
from contextlib import ExitStack

import numpy as np

import concourse.bass as bass
from concourse import mybir

F32 = mybir.dt.float32
ALU = mybir.AluOpType
ACT = mybir.ActivationFunctionType
AX = mybir.AxisListType.X

P = 128
TC = 512
NJ = TC // P
LN_EPS = 1e-5
RMS_EPS = float(np.finfo(np.float32).eps)
A_FLOOR = 1e-4
MAGIC = float(1.5 * 2 ** 23)
SCAN_TABLE = "natural_log_exp_and_others"
DVE_PAIRS = ((1, 3), (4, 6), (1, 4), (1, 3, 6))


class Count:

    def __init__(self, sem):
        self.sem, self.value = sem, 0

    def up(self, n):
        self.value += n
        return (self.sem, self.value)


class Queue:

    def __init__(self):
        self.items, self.seen = [], {}

    def put(self, make, after=(), done=None, n=1):
        waits = []
        for t in after:
            if t is None:
                continue
            sem, value = t
            if self.seen.get(sem.name, 0) < value:
                self.seen[sem.name] = value
                waits.append(t)
        self.items.append((waits, make, done.sem if done else None, n))
        return done.up(n) if done else None

    def run(self, engine):
        for waits, make, sem, n in self.items:
            for s, value in waits:
                engine.wait_ge(s, value)
            ins = make(engine)
            if sem is not None:
                ins.then_inc(sem, n)


def block_kernel(nc, x, w_in, w_x, w_dt, b_dt, a_log, bc_bias, bc_norm, freqs, d_skip, w_out,
                 ln1_g, ln1_b, w1, b1, ln2_g, ln2_b, w2, b2, ident_in, tri_in, out, rows_dram):
    T, DM = x.shape
    KD = DM // P
    E = w_out.shape[1] * P
    KE = E // P
    NS = a_log.shape[2]
    NF = NS // 2
    HID = w1.shape[2]
    KH = HID // P
    NCH = T // TC
    PER_BATCH = NCH // 2
    HALF = TC // 2
    NROW = 2 * NS + 2
    LAM, NCB = 2 * NS, 2 * NS + 1
    DT_SLOTS = KE + 2
    N_SLOTS = 9
    RING = 7
    U_AHEAD = 2
    DA_BANKS = 3
    PE_PAIR = NS // 2 - 1
    LAST_UP = 42
    GATE_AT = 2
    C1 = 6.28125
    C2 = float(np.float32(int((2 * np.pi - C1) * 2 ** 20)) / 2 ** 20)
    C3 = float(2 * np.pi - C1 - C2)
    PI = 3.1415925

    with ExitStack() as ctx:
        total = [0]

        def sb(name, shape, dt=F32):
            total[0] += int(np.prod(shape[1:])) * 4
            return ctx.enter_context(nc.sbuf_tensor(name, shape, dt))

        def psum(name):
            return ctx.enter_context(nc.psum_tensor(name, [P, 512], F32))

        def count(name):
            return Count(ctx.enter_context(nc.semaphore(name)))

        ident = sb("ident", [P, P])
        tri = sb("tri", [P, P])
        ones = sb("ones", [P, P])
        w_in_sb = sb("w_in_sb", [P, KD, 2 * E])
        w_x_sb = sb("w_x_sb", [P, KE, 2 * NS + 2])
        w_out_sb = sb("w_out_sb", [P, KE, DM])
        w1_sb = sb("w1_sb", [P, KD, HID])
        w2_sb = sb("w2_sb", [P, KH, DM + 1])
        w_dt_sb = sb("w_dt_sb", [P, KE])
        b_dt_sb = sb("b_dt_sb", [P, KE])
        d_sb = sb("d_sb", [P, KE])
        a_sb = sb("a_sb", [P, KE, NS])
        bc_bias_sb = sb("bc_bias_sb", [P, NS, 2])
        bc_norm_sb = sb("bc_norm_sb", [P, NS, 2])
        freq_sb = sb("freq_sb", [P, NF])
        ln1_g_sb = sb("ln1_g_sb", [P, KD])
        ln1_b_sb = sb("ln1_b_sb", [P, KD])
        b1_sb = sb("b1_sb", [P, KH])
        ln2_g_sb = sb("ln2_g_sb", [P, KH])
        ln2_b_sb = sb("ln2_b_sb", [P, KH])
        bias_w2 = sb("bias_w2", [P, DM])
        ln_eps = sb("ln_eps", [P, 1])
        rms_eps = sb("rms_eps", [P, 1])
        inv_e = sb("inv_e", [P, 1])
        tern = sb("tern", [P, 4])
        stage = sb("stage", [P, NJ, DM])
        stats = sb("stats", [P, NJ, 6])
        mv = sb("mv", [P, NJ, 2])
        rstd = sb("rstd", [P, NJ])
        newton = sb("newton", [P, 2 * NJ])
        xn_t = sb("xn_t", [P, KD, TC])
        xp_last = sb("xp_last", [P, 2, KE])
        zs = sb("zs", [P, NJ, E])
        wide = sb("wide", [P, KE * TC])
        dt = sb("dt", [P, DT_SLOTS, TC])
        ssm = sb("ssm", [P, NJ, 2 * NS + 2])
        mdt = sb("mdt", [P, NJ])
        before = sb("before", [P, 2, NJ + 1])
        ang = sb("ang", [P, NJ, NF])
        turn = sb("turn", [P, NJ, 2, NF])
        rem = sb("rem", [P, NJ, 2, NF])
        sc = sb("sc", [P, NJ, 2, NF])
        bc = sb("bc", [P, NJ, NS, 2])
        bc_sq = sb("bc_sq", [P, NJ, NS, 2])
        ms = sb("ms", [P, NJ, 2])
        rms = sb("rms", [P, NJ, 2])
        rope_a = sb("rope_a", [P, NJ, NF, 2])
        rope_b = sb("rope_b", [P, NJ, NF, 2])
        lam_e = sb("lam_e", [P, NJ])
        lam_bc = sb("lam_bc", [P, TC])
        ncb_bc = sb("ncb_bc", [P, TC])
        bcb = sb("bcb", [P, NS, 2, TC])
        b_last = sb("b_last", [P, NS])
        b_cols = sb("b_cols", [P, NJ, 2])
        r_dt = sb("r_dt", [P, TC])
        late = sb("late", [P, 1])
        slots = sb("slots", [P, N_SLOTS, TC])
        ring = sb("ring", [P, RING, 2, TC])
        state = sb("state", [P, KE, NS])
        gated = sb("gated", [P, NJ, P])
        rows_tm = gated
        yg = sb("yg", [P, KE, TC])
        x2 = sb("x2", [P, NJ, DM])
        h_t = sb("h_t", [P, KD, TC])
        small = {of: (sb("stats_" + of, [P, NJ, 6]), sb("mv_" + of, [P, NJ, 2]), sb("rstd_" + of, [P, NJ]),
                      sb("newton_" + of, [P, 2 * NJ]), sb("nmr_" + of, [P, NJ]))
                 for of in ("attn", "hidden", "last")}
        hidden = wide[:, :].rearrange("p (m t) -> p m t", m=KH)
        last_hidden = ring[:, 0:2, :, :].rearrange("p r a (s t) -> p (r a s) t", t=HALF)

        psum_da = [psum(f"psum_da{i}") for i in range(DA_BANKS)]
        psum_y = psum("psum_y")
        psum_f = [psum(f"psum_f{i}") for i in range(4)]

        names = []
        names += "c_const c_const_ffn c_xin c_xres c_lamld c_blast_pe".split()
        names += "c_setup c_wprep c_actprep c_peprep".split()
        names += "c_stat c_rstd_a c_rstd c_norm c_xt c_xt_ev".split()
        names += "c_proj c_silu c_zproj c_zsilu c_ssm".split()
        names += "c_dtp c_soft c_dt c_mdt c_mdt_sb c_cum c_ang c_sin".split()
        names += "c_bc c_lam_a c_rope c_rowt c_row_ev c_row_st".split()
        names += "c_wq c_wt c_wt_ev c_diag c_u_pe c_blast".split()
        names += "c_da c_u c_scan c_p_pool c_p_dve c_y".split()
        names += "c_gate c_gt c_gt_ev c_out".split()
        names += "c_stat2 c_rstd2_a c_rstd2 c_on c_x2 c_h c_ht c_ht_ev c_res c_store".split()
        names += "c_f1 c_up_ev c_gelu c_f2 c_sq c_ffn".split()
        k = {name: count(name) for name in names}
        c_piece = [count(f"c_piece{n}") for n in range(NS)]
        pe, act, dve, pool, sp = (Queue() for _ in range(5))

        free_banks = [(i, None) for i in range(4)]

        def take():
            while not free_banks:
                yield 1
            return free_banks.pop(0)

        def take_slot():
            while not free_slots:
                yield 1
            return free_slots.pop(0)

        def give(i, token):
            free_banks.append((i, token))

        free_slots = [(i, None) for i in range(N_SLOTS)]

        load_x_first = sp.put(lambda e: e.dma_start(stage[:, :, :], x[0:TC, :].rearrange("(j p) d -> p j d", p=P)),
                              (), k["c_xin"], 16)
        loads = [(ident, ident_in), (w_in_sb, w_in), (w_x_sb, w_x), (w_dt_sb, w_dt), (b_dt_sb, b_dt),
                 (tri, tri_in), (d_sb, d_skip), (a_sb, a_log)]
        def ap_of(t):
            return t[tuple(slice(None) for _ in t.shape)]
        for dst, src in loads:
            loaded = sp.put(lambda e, d=dst, s=src: e.dma_start(ap_of(d), s), done=k["c_const"], n=16)
        for dst, src in ((bc_bias_sb[:, :, :], bc_bias), (bc_norm_sb[:, :, :], bc_norm)):
            loaded = sp.put(lambda e, d=dst, s=src: e.dma_start(d, s.partition_broadcast(P)), done=k["c_const"], n=16)
        loaded = sp.put(lambda e: e.dma_start(freq_sb[:, :], freqs.partition_broadcast(P)), done=k["c_const"], n=16)
        for dst, src in ((w_out_sb, w_out), (w1_sb, w1), (ln1_g_sb, ln1_g), (ln1_b_sb, ln1_b), (b1_sb, b1),
                         (ln2_g_sb, ln2_g), (ln2_b_sb, ln2_b)):
            sp.put(lambda e, d=dst, s=src: e.dma_start(ap_of(d), s), done=k["c_const_ffn"], n=16)
        sp.put(lambda e: e.dma_start(w2_sb[:, :, 0:DM], w2), done=k["c_const_ffn"], n=16)
        loaded_ffn = sp.put(lambda e: e.dma_start(bias_w2[:, :], b2.partition_broadcast(P)),
                            done=k["c_const_ffn"], n=16)

        ones_set = dve.put(lambda e: e.memset(ones[:, :], 1.0), done=k["c_setup"])
        dve.put(lambda e: e.memset(ln_eps[:, :], LN_EPS), done=k["c_setup"])
        dve.put(lambda e: e.memset(rms_eps[:, :], RMS_EPS), done=k["c_setup"])
        dve.put(lambda e: e.memset(rows_tm[:, :, :], 0.0), done=k["c_setup"])
        consts_set = dve.put(lambda e: e.memset(inv_e[:, :], 1.0 / E), done=k["c_setup"])

        act.put(lambda e: e.preload_act_table_set(SCAN_TABLE))
        a_exp = act.put(lambda e: e.activation(a_sb[:, :, :], a_sb[:, :, :], ACT.Exp), (loaded,), k["c_actprep"])
        a_ready = dve.put(lambda e: e.tensor_scalar(a_sb[:, :, :], a_sb[:, :, :], -1.0, -A_FLOOR, ALU.mult, ALU.min),
                          (a_exp, loaded), k["c_wprep"])
        f0 = act.put(lambda e: e.activation(ang[:, 0, :], freq_sb[:, :], ACT.Abs), (), k["c_actprep"])
        f1 = act.put(lambda e: e.activation(ang[:, 1, :], ang[:, 0, :], ACT.Exp, scale=-1.0), (f0,), k["c_actprep"])
        f2 = act.put(lambda e: e.activation(ang[:, 2, :], ang[:, 1, :], ACT.Ln, bias=1.0), (f1,), k["c_actprep"])
        f3 = act.put(lambda e: e.activation(ang[:, 3, :], freq_sb[:, :], ACT.Relu), (), k["c_actprep"])
        freq_ready = dve.put(lambda e: e.tensor_tensor(freq_sb[:, :], ang[:, 2, :], ang[:, 3, :], ALU.add),
                             (f3,), k["c_wprep"])

        def ternary(wt, elements, n, after):
            copy = wide[:, :].rearrange("p (a b) -> p a b", a=n)
            a = act.put(lambda e: e.activation(copy, wt, ACT.Abs, accum_out=tern[:, 0:1]), (loaded_ffn, after),
                        k["c_actprep"])
            bank, fr = yield from take()
            yield 1
            b = pe.put(lambda e: e.matmul(psum_f[bank][:, 0:1], ones[:, :], tern[:, 0:1], start=True, stop=True),
                       (a, consts_set, fr), k["c_peprep"])
            yield 1
            d = k["c_wprep"]
            t = dve.put(lambda e: e.tensor_scalar(tern[:, 1:2], psum_f[bank][:, 0:1], 1.0 / elements, 1e-5, ALU.mult,
                                                  ALU.max), (b,), d)
            give(bank, t)
            t = dve.put(lambda e: e.reciprocal(tern[:, 2:3], tern[:, 1:2]), (t,), d)
            t = dve.put(lambda e: e.reciprocal(tern[:, 3:4], tern[:, 2:3]), (t,), d)
            t = dve.put(lambda e: e.tensor_scalar(copy, wt, tern[:, 2:3], MAGIC, ALU.mult, ALU.add), (t, a), d)
            yield 1
            t = dve.put(lambda e: e.tensor_scalar(copy, copy, MAGIC, 1.0, ALU.subtract, ALU.min), (t,), d)
            yield 1
            t = dve.put(lambda e: e.tensor_scalar(copy, copy, -1.0, tern[:, 3:4], ALU.max, ALU.mult), (t,), d)
            yield 1
            t = dve.put(lambda e: e.tensor_tensor(copy, copy, wt, ALU.subtract), (t,), d)
            yield 1
            return dve.put(lambda e: e.tensor_tensor(wt, wt, copy, ALU.add), (t,), d)

        def prepare_ffn(c):
            mean_w2 = wide[:, 0:DM]
            if c:
                return
            d = k["c_wprep"]
            t = yield from ternary(w1_sb[:, :, :], DM * HID, KD, None)
            yield 2
            t = yield from ternary(w2_sb[:, :, 0:DM], DM * HID, KH, t)
            yield 1
            for m in range(KH):
                t2 = dve.put(lambda e, m=m: e.tensor_scalar(wide[:, m * P:(m + 1) * P], ones[:, :],
                                                            ln2_b_sb[:, m:m + 1], None, ALU.mult), (t,), d)
            yield 3
            bank, fr = yield from take()
            for m in range(KH):
                b = pe.put(lambda e, m=m: e.matmul(psum_f[bank][:, 0:DM], wide[:, m * P:(m + 1) * P],
                                                   w2_sb[:, m, 0:DM], start=m == 0, stop=m == KH - 1), (t2, fr),
                           k["c_peprep"])
            yield 1
            t = dve.put(lambda e: e.tensor_tensor(bias_w2[:, :], bias_w2[:, :], psum_f[bank][:, 0:DM], ALU.add), (b,),
                        d)
            for m in range(KH):
                t = dve.put(lambda e, m=m: e.tensor_scalar(w2_sb[:, m, 0:DM], w2_sb[:, m, 0:DM], ln2_g_sb[:, m:m + 1],
                                                           None, ALU.mult), (b, t), d)
                if m % 2:
                    yield 1
            t = dve.put(lambda e: e.memset(w2_sb[:, :, DM:DM + 1], 1.0 / HID), (), d)
            for m in range(KH):
                b = pe.put(lambda e, m=m: e.matmul(psum_f[bank][:, 0:DM], ones[:, :], w2_sb[:, m, 0:DM],
                                                   start=m == 0, stop=m == KH - 1), (t,), k["c_peprep"])
            yield 1
            t = dve.put(lambda e: e.tensor_scalar(mean_w2, psum_f[bank][:, 0:DM], 1.0 / HID, None, ALU.mult), (b,), d)
            give(bank, t)
            for m in range(KH):
                t = dve.put(lambda e, m=m: e.tensor_tensor(w2_sb[:, m, 0:DM], w2_sb[:, m, 0:DM], mean_w2,
                                                           ALU.subtract), (t,), d)
            R["ffn_ready"] = t

        S = [dict() for _ in range(NCH)]

        def first(c):
            return c % PER_BATCH == 0

        def rsqrt(var, y, tmp, eps, scale, after, c_a, c_d):
            t1, t2 = tmp
            yield 1
            a = act.put(lambda e: e.activation(t1, var, ACT.Ln, bias=eps[:, :], scale=scale), after, c_a)
            a = act.put(lambda e: e.activation(y, t1, ACT.Exp, scale=-0.5), (a,), c_a)
            eps_v = LN_EPS if eps is ln_eps else RMS_EPS
            yield 2
            d = dve.put(lambda e: e.tensor_tensor(t1, y, y, ALU.mult), (a,), c_d)
            d = dve.put(lambda e: e.scalar_tensor_tensor(out=t1, in0=var, scalar=eps_v / scale, in1=t1, op0=ALU.add,
                                                         op1=ALU.mult), (d,), c_d)
            d = dve.put(lambda e: e.tensor_scalar(t1, t1, -0.5 * scale, 1.5, ALU.mult, ALU.add), (d,), c_d)
            return dve.put(lambda e: e.tensor_tensor(y, y, t1, ALU.mult), (d,), c_d)

        def load_x(c):
            if c == 0:
                S[c]["x"] = load_x_first
                return
            S[c]["x"] = sp.put(lambda e: e.dma_start(stage[:, :, :], x[c * TC:(c + 1) * TC, :].rearrange(
                "(j p) d -> p j d", p=P)), tuple(R.get("stage_free", ())), k["c_xin"], 16)

        def norm_x(c):
            for j in range(NJ):
                t = dve.put(lambda e, j=j: e.bn_stats(stats[:, j, :], stage[:, j, :]), (S[c]["x"],), k["c_stat"])
            for j in range(NJ):
                t = dve.put(lambda e, j=j: e.bn_aggr(mv[:, j, :], stats[:, j, :]), (t,), k["c_stat"])
            r = yield from rsqrt(mv[:, :, 1], rstd[:, :], (newton[:, 0:NJ], newton[:, NJ:]), ln_eps, 1.0,
                                 (t, consts_set), k["c_rstd_a"], k["c_rstd"])
            for j in range(NJ):
                t = dve.put(lambda e, j=j: e.tensor_scalar(stage[:, j, :], stage[:, j, :], mv[:, j, 0:1],
                                                           rstd[:, j:j + 1], ALU.subtract, ALU.mult),
                            (r,), k["c_norm"])
            S[c]["xn"] = t

        def transpose_x(c):
            S[c]["xt"] = []
            for i in range(KD):
                b, fr = yield from take()
                for j in range(NJ):
                    t = pe.put(lambda e, i=i, j=j, b=b: e.transpose(psum_f[b][:, j * P:(j + 1) * P],
                                                                   stage[:, j, i * P:(i + 1) * P], ident[:, :]),
                               (S[c]["xn"], fr, loaded), k["c_xt"])
                S[c]["xt"].append((b, t))
                R["stage_free"] = [t]
                yield 1
            for i, (b, t) in enumerate(S[c]["xt"]):
                t = act.put(lambda e, i=i, b=b: e.copy(xn_t[:, i, :], psum_f[b][:, :]), (t, R.get("zproj")),
                            k["c_xt_ev"])
                give(b, t)
            S[c]["xnt"] = t

        def project_x(c):
            S[c]["proj"] = []
            for m in range(KE):
                b, fr = yield from take()
                for i in range(KD):
                    t = pe.put(lambda e, i=i, m=m, b=b: e.matmul(psum_f[b][:, :], w_in_sb[:, i, m * P:(m + 1) * P],
                                                                xn_t[:, i, :], start=i == 0, stop=i == KD - 1),
                               (S[c]["xnt"], fr, loaded), k["c_proj"])
                S[c]["proj"].append((b, t))
                yield 1
            yield 1
            for m, (b, t) in enumerate(S[c]["proj"]):
                xs, free = yield from take_slot()
                S[c]["xs", m] = xs
                t = act.put(lambda e, b=b, xs=xs: e.activation(slots[:, xs, :], psum_f[b][:, :], ACT.Silu),
                            (t,) + (free or ()), k["c_silu"])
                give(b, t)
            act.put(lambda e: e.preload_act_table_set(SCAN_TABLE))
            S[c]["xp"] = t

        def project_z(c):
            S[c]["zproj"] = []
            for j in range(NJ):
                b, fr = yield from take()
                for i in range(KD):
                    t = pe.put(lambda e, i=i, j=j, b=b: e.matmul(psum_f[b][:, :], xn_t[:, i, j * P:(j + 1) * P],
                                                                w_in_sb[:, i, E:2 * E], start=i == 0,
                                                                stop=i == KD - 1),
                               (S[c]["xnt"], fr), k["c_zproj"])
                S[c]["zproj"].append((b, t))
                yield 1
            R["zproj"] = t
            yield 1
            for j, (b, t) in enumerate(S[c]["zproj"]):
                t = act.put(lambda e, j=j, b=b: e.activation(zs[:, j, :], psum_f[b][:, :], ACT.Silu),
                            (t, R.get("gate")), k["c_zsilu"])
                give(b, t)
            act.put(lambda e: e.preload_act_table_set(SCAN_TABLE))
            S[c]["zs"] = t

        def project_dt(c):
            b, fr = yield from take()
            for m in range(KE):
                t = pe.put(lambda e, m=m, b=b: e.matmul(psum_f[b][:, :], w_x_sb[:, m, 2 * NS:2 * NS + 1]
                                                       .broadcast_to([P, P]), slots[:, S[c]["xs", m], :],
                                                       start=m == 0, stop=m == KE - 1),
                           (S[c]["xp"], fr), k["c_dtp"])
            S[c]["dtp"] = (b, t)
            yield 1
            b, fr = yield from take()
            for j in range(NJ):
                for m in range(KE):
                    t = pe.put(lambda e, j=j, m=m, b=b: e.matmul(
                        psum_f[b][:, j * NROW:(j + 1) * NROW],
                        slots[:, S[c]["xs", m], j * P:(j + 1) * P], w_x_sb[:, m, :],
                        start=m == 0, stop=m == KE - 1), (fr,), k["c_ssm"])
            S[c]["ssm_pe"] = t
            S[c]["ssm"] = (b, t)

        def slot(c, m):
            return (KE * c + m) % DT_SLOTS

        def softplus_dt(c):
            b, t = S[c]["dtp"]
            ca = k["c_soft"]
            halves = []

            def add_halves(m, z, a):
                S[c]["dt", m] = d = dve.put(lambda e: e.tensor_tensor(
                    dt[:, slot(c, m), :], dt[:, slot(c, m), :], slots[:, z, :], ALU.add), (a,), k["c_dt"])
                free_slots.append((z, (d,)))

            for m in range(KE):
                z, free = yield from take_slot()
                second = slots[:, z, :]
                a = act.put(lambda e, m=m, second=second: e.activation(second, psum_f[b][:, :], ACT.Abs,
                                                                       scale=w_dt_sb[:, m:m + 1],
                                                                       bias=b_dt_sb[:, m:m + 1]),
                            (t,) + (free or ()), ca)
                a = act.put(lambda e, second=second: e.activation(second, second, ACT.Exp, scale=-1.0), (a,), ca)
                yield 1
                a = act.put(lambda e, second=second: e.activation(second, second, ACT.Ln, bias=1.0), (a,), ca)
                a = act.put(lambda e, m=m: e.activation(dt[:, slot(c, m), :], psum_f[b][:, :], ACT.Relu,
                                                        scale=w_dt_sb[:, m:m + 1], bias=b_dt_sb[:, m:m + 1]),
                            (t, R.get("wq"), R.get("mdt_pe")), ca)
                halves.append((m, z, a))
                yield 1
                if m:
                    add_halves(*halves[m - 1])
            give(b, a)
            yield 1
            add_halves(*halves[-1])
            S[c]["dt"] = S[c]["dt", KE - 1]

        def mean_dt(c):
            b, fr = S[c]["sums"] = yield from take()
            at = 0
            for j in range(NJ):
                for m in range(KE):
                    t = pe.put(lambda e, j=j, m=m: e.matmul(psum_f[b][:, at + j:at + j + 1],
                                                            dt[:, slot(c, m), j * P:(j + 1) * P], inv_e[:, :],
                                                            start=m == 0, stop=m == KE - 1),
                               (S[c]["dt"], fr), k["c_mdt"])
            R["mdt_pe"] = t
            S[c]["mdt"] = t

        def sums_dt(c):
            b, _ = S[c]["sums"]
            at = 0
            now, old = before[:, c % 2, :], before[:, 1 - c % 2, :]
            cd = k["c_mdt_sb"]
            if first(c):
                d = dve.put(lambda e: e.memset(now[:, 0:1], 0.0), (R.get("cum"),), cd)
            else:
                d = dve.put(lambda e: e.tensor_copy(now[:, 0:1], old[:, NJ:NJ + 1]), (R.get("cum"),), cd)
            d = dve.put(lambda e: e.tensor_copy(mdt[:, :], psum_f[b][:, at:at + NJ]), (S[c]["mdt"],), cd)
            d = dve.put(lambda e: e.tensor_tensor_scan(now[:, 1:NJ + 1], ones[:, 0:NJ], mdt[:, :], now[:, 0:1],
                                                       ALU.mult, ALU.add), (d,), cd)
            pe.put(lambda e: e.matmul(psum_f[b][:, at + NJ:at + 2 * NJ], tri[:, :], mdt[:, :], start=True,
                                      stop=False), (d,))
            R["cum"] = S[c]["cum"] = pe.put(
                lambda e: e.matmul(psum_f[b][:, at + NJ:at + 2 * NJ], ones[:, :], now[:, 0:NJ], start=False,
                                   stop=True), (d,), k["c_cum"])

        def bc_norms(c):
            b, t = S[c]["ssm"]
            cd = k["c_bc"]
            d = S[c]["ssm_sb"] = dve.put(lambda e: e.tensor_copy(
                ssm[:, :, :], psum_f[b][:, 0:NJ * NROW].rearrange("p (j r) -> p j r", j=NJ)), (t, R.get("lam_a")), cd)
            give(b, d)
            bias = bc_bias_sb[:, :, :].rearrange("p n a -> p (n a)").unsqueeze(1).broadcast_to([P, NJ, 2 * NS])
            flat = bc[:, :, :, :].rearrange("p j n a -> p j (n a)")
            d = dve.put(lambda e: e.tensor_tensor(flat, ssm[:, :, 0:2 * NS], bias, ALU.add),
                        (d,), cd)
            d = dve.put(lambda e: e.tensor_tensor(bc_sq[:, :, :, :], bc[:, :, :, :], bc[:, :, :, :], ALU.mult),
                        (d,), cd)
            for a in range(2):
                d = dve.put(lambda e, a=a: e.tensor_reduce(ms[:, :, a], bc_sq[:, :, :, a], AX, ALU.add), (d,), cd)
            S[c]["ms"] = d
            yield 3
            R["lam_a"] = S[c]["lam_a"] = act.put(
                lambda e: e.activation(lam_e[:, :], ssm[:, :, 2 * NS + 1], ACT.Exp, scale=-1.0),
                (S[c]["ssm_sb"], R.get("lam_free")), k["c_lam_a"])
            S[c]["rms"] = yield from rsqrt(ms[:, :, :], rms[:, :, :],
                                           (rope_a[:, :, 0, :], rope_b[:, :, 0, :]), rms_eps, 1.0 / NS, (d,),
                                           k["c_lam_a"], k["c_bc"])

        def angles(c):
            b, _ = S[c]["sums"]
            at = 0
            cum = psum_f[b][:, at + NJ:at + 2 * NJ].unsqueeze(2).broadcast_to([P, NJ, NF])
            fr = freq_sb[:, :].unsqueeze(1).broadcast_to([P, NJ, NF])
            cd = k["c_ang"]
            d = dve.put(lambda e: e.tensor_tensor(ang[:, :, :], cum, fr, ALU.mult), (S[c]["cum"], R.get("sin")), cd)
            give(b, d)
            for a, off in ((0, 0.0), (1, 0.25)):
                d2 = dve.put(lambda e, a=a, off=off: e.tensor_scalar(turn[:, :, a, :], ang[:, :, :],
                                                                     float(1 / (2 * np.pi)), off, ALU.mult, ALU.add),
                             (d,), cd)
            d = dve.put(lambda e: e.tensor_scalar(turn[:, :, :, :], turn[:, :, :, :], MAGIC, MAGIC, ALU.add,
                                                  ALU.subtract), (d2,), cd)
            d = dve.put(lambda e: e.tensor_scalar(turn[:, :, 1, :], turn[:, :, 1, :], -0.25, None, ALU.add), (d,), cd)
            for a in range(2):
                d2 = dve.put(lambda e, a=a: e.scalar_tensor_tensor(out=rem[:, :, a, :], in0=turn[:, :, a, :],
                                                                   scalar=-C1, in1=ang[:, :, :], op0=ALU.mult,
                                                                   op1=ALU.add), (d,), cd)
            flat_t = turn[:, :, :, :].rearrange("p j a f -> p (j a f)")
            flat_r = rem[:, :, :, :].rearrange("p j a f -> p (j a f)")
            for part in (C2, C3):
                d2 = dve.put(lambda e, part=part: e.scalar_tensor_tensor(out=flat_r, in0=flat_t, scalar=-part,
                                                                         in1=flat_r, op0=ALU.mult, op1=ALU.add),
                             (d2,), cd)
            S[c]["ang"] = dve.put(lambda e: e.tensor_scalar(flat_r, flat_r, -PI, PI, ALU.max, ALU.min), (d2,), cd)

        def sines(c):
            R["sin"] = S[c]["sin"] = act.put(lambda e: e.activation(sc[:, :, :, :], rem[:, :, :, :], ACT.Sin),
                                            (S[c]["ang"], R.get("rope")), k["c_sin"])
            act.put(lambda e: e.preload_act_table_set(SCAN_TABLE))

        def rope(c):
            cd = k["c_rope"]
            d = S[c]["rms"]
            for a in range(2):
                d = dve.put(lambda e, a=a: e.tensor_tensor(
                    bc[:, :, :, a], bc[:, :, :, a], rms[:, :, a:a + 1].broadcast_to([P, NJ, NS]), ALU.mult), (d,), cd)
            flat = bc[:, :, :, :].rearrange("p j n a -> p j (n a)")
            nw = bc_norm_sb[:, :, :].rearrange("p n a -> p (n a)").unsqueeze(1).broadcast_to([P, NJ, 2 * NS])
            d0 = dve.put(lambda e: e.tensor_tensor(flat, flat, nw, ALU.mult), (d,), cd)
            pairs = bc[:, :, :, :].rearrange("p j (f o) a -> p j f o a", o=2)
            even, odd = pairs[:, :, :, 0, :], pairs[:, :, :, 1, :]
            rows = rows_tm[:, :, 0:2 * NS].rearrange("p j (f o a) -> p j f o a", o=2, a=2)
            sin = sc[:, :, 0, :].unsqueeze(3).broadcast_to([P, NJ, NF, 2])
            cos = sc[:, :, 1, :].unsqueeze(3).broadcast_to([P, NJ, NF, 2])
            for which, (fa, fb, op) in enumerate(((cos, sin, ALU.subtract), (sin, cos, ALU.add))):
                dve.put(lambda e, fa=fa: e.tensor_tensor(rope_a[:, :, :, :], even, fa, ALU.mult),
                        (S[c]["sin"], d0, d if which else None), cd)
                d = dve.put(lambda e, fb=fb: e.tensor_tensor(rope_b[:, :, :, :], odd, fb, ALU.mult), (), cd)
                d = dve.put(lambda e, which=which, op=op: e.tensor_tensor(rows[:, :, :, which, :],
                                                                          rope_a[:, :, :, :], rope_b[:, :, :, :], op),
                            (d, R.get("gt")), cd)
            pe_b = rows_tm[:, :, 4 * PE_PAIR:4 * PE_PAIR + 4].rearrange("p j (n a) -> p j n a", a=2)[:, :, :, 0]
            S[c]["b_cols"] = dve.put(lambda e: e.tensor_copy(b_cols[:, :, :], pe_b), (d, R.get("diag")), cd)
            made = rows_tm[:, :, 0:2 * NS].rearrange("p j (n a) -> p j n a", a=2)
            d = dve.put(lambda e: e.tensor_tensor(bc_sq[:, :, :, 0], made[:, :, :, 0], made[:, :, :, 1], ALU.mult),
                        (d,), cd)
            d = dve.put(lambda e: e.tensor_reduce(newton[:, 0:NJ], bc_sq[:, :, :, 0], AX, ALU.add), (d,), cd)
            d = dve.put(lambda e: e.tensor_scalar(rows_tm[:, :, NCB], newton[:, 0:NJ], -1.0, None, ALU.mult), (d,),
                        cd)
            d = dve.put(lambda e: e.tensor_scalar(lam_e[:, :], lam_e[:, :], 1.0, None, ALU.add), (S[c]["lam_a"],), cd)
            d = dve.put(lambda e: e.reciprocal(rows_tm[:, :, LAM], lam_e[:, :]), (d,), cd)
            if first(c):
                d = dve.put(lambda e: e.memset(rows_tm[0:1, 0, LAM:LAM + 1], 1.0), (d,), cd)
            R["rope"] = R["lam_free"] = S[c]["rope"] = d

        def transpose_rows(c):
            b, fr = yield from take()
            for j in range(NJ):
                t = pe.put(lambda e, j=j, b=b: e.transpose(psum_f[b][:, j * P:(j + 1) * P], rows_tm[:, j, :],
                                                          ident[:, :]), (S[c]["rope"], fr), k["c_rowt"])
            R["gt"] = t
            yield 2
            z, free = yield from take_slot()
            t = act.put(lambda e: e.copy(slots[0:NROW, z, :], psum_f[b][0:NROW, :]), (t,) + (free or ()),
                        k["c_row_ev"])
            give(b, t)
            S[c]["row_st"] = sp.put(lambda e: e.dma_start(rows_dram[c], slots[0:NROW, z, :]), (t,),
                                    k["c_row_st"], 16)
            free_slots.append((z, (S[c]["row_st"],)))

        def load_lam(c):
            for dst, row in ((lam_bc, LAM), (ncb_bc, NCB)):
                t = sp.put(lambda e, dst=dst, row=row: e.dma_start(
                    dst[:, :], rows_dram[c][row, :].partition_broadcast(P)),
                           (S[c]["row_st"], R.get("wq")), k["c_lamld"], 16)
            S[c]["lam"] = t

        def load_pieces(c):
            for i in range(NS // 2):
                load_piece(c, 2 * i)
                load_piece(c, 2 * i + 1)
                if c and i + 1 < NS // 2:
                    yield 2

        def load_piece(c, n):
            assert c == 0 or R["last of", n // 2] == (c - 1, KE - 1)
            if n // 2 == PE_PAIR:
                dst, src = bcb[:, n, 1, :], rows_dram[c][2 * n + 1, :]
            else:
                dst, src = bcb[:, n, :, :], rows_dram[c][2 * n:2 * n + 2, :]
            S[c][f"piece{n}"] = sp.put(
                lambda e: e.dma_start(dst, src.partition_broadcast(P)),
                (S[c]["row_st"], R.get(("u", n // 2)), R.get(("p", n // 2)), R.get("b_last")), c_piece[n], 16)

        def make_diagonals(c):
            for a in range(2):
                for j in range(NJ):
                    t = act.put(lambda e, a=a, j=j: e.activation(
                        bcb[:, 2 * PE_PAIR + a, 0, j * P:(j + 1) * P], ident[:, :], ACT.Identity,
                        scale=b_cols[:, j, a:a + 1]), (S[c]["b_cols"], R.get("u_pe")), k["c_diag"])
                yield 1
            R["diag"] = S[c]["diag"] = t

        def transpose_w(c, m):
            b, fr = yield from take()
            ws = S[c]["ws", m]
            for j in range(NJ):
                t = pe.put(lambda e, j=j: e.transpose(psum_f[b][:, j * P:(j + 1) * P],
                                                      slots[:, ws, j * P:(j + 1) * P], ident[:, :]),
                           (S[c][f"w{m}"], fr), k["c_wt"])
            S[c]["w_transposed", m] = t
            yield 1
            z, free = yield from take_slot()
            S[c]["wt_slot", m] = z
            S[c]["wt", m] = t = act.put(lambda e: e.copy(slots[:, z, :], psum_f[b][:, :]), (t,) + (free or ()),
                                        k["c_wt_ev"])
            give(b, t)

        def make_wq(c, m):
            cd = k["c_wq"]
            d_ = dt[:, slot(c, m), :]
            xs = S[c]["xs", m]
            ws, w_free = yield from take_slot()
            qs, q_free = yield from take_slot()
            S[c]["ws", m], S[c]["qs", m] = ws, qs
            dve.put(lambda e: e.tensor_copy(xp_last[:, c % 2, m:m + 1], slots[:, xs, TC - 1:TC]),
                    (S[c]["xp"], R.get("wq")), cd)
            after = (S[c]["lam"], S[c]["dt", m], S[c]["xp"], R.get("wq"))
            w_, q_, x_ = slots[:, ws, :], slots[:, qs, :], slots[:, xs, :]
            d = dve.put(lambda e: e.tensor_tensor(w_, lam_bc[:, :], d_, ALU.mult), after + (w_free or ()), cd)
            d = dve.put(lambda e: e.tensor_tensor(r_dt[:, :], d_, w_, ALU.subtract), (d,), cd)
            if not first(c):
                t = dve.put(lambda e: e.tensor_tensor(late[:, :], r_dt[:, 0:1], xp_last[:, (c - 1) % 2, m:m + 1],
                                                      ALU.mult), (d,), cd)
                S[c][f"state{m}"] = dve.put(lambda e: e.scalar_tensor_tensor(
                    out=state[:, m, :], in0=b_last[:, :], scalar=late[:, :], in1=state[:, m, :], op0=ALU.mult,
                    op1=ALU.add), (t, R["b_last"], R["b_last_pe"], R.get(("state", m))), cd)
            yield 1
            d = dve.put(lambda e: e.tensor_tensor(w_[:, 0:TC - 1], w_[:, 0:TC - 1], r_dt[:, 1:TC], ALU.add), (d,), cd)
            S[c][f"w{m}"] = d = dve.put(lambda e: e.tensor_tensor(w_, w_, x_, ALU.mult), (d,), cd)
            yield 2
            dve.put(lambda e: e.memset(q_[:, TC - 1:TC], 0.0), q_free or (), cd)
            d = dve.put(lambda e: e.tensor_tensor(q_[:, 0:TC - 1], ncb_bc[:, 0:TC - 1], r_dt[:, 1:TC], ALU.mult),
                        (d,), cd)
            d = dve.put(lambda e: e.scalar_tensor_tensor(out=q_, in0=q_, scalar=d_sb[:, m:m + 1], in1=x_, op0=ALU.add,
                                                         op1=ALU.mult), (d,), cd)
            R["wq"] = S[c][f"q{m}"] = d
            free_slots.append((xs, (d, S[c]["ssm_pe"])))

        def after_pair(c, m, i, n):
            at = (c * KE + m) * (NS // 2) + i + n
            return (at // (KE * NS // 2), at // (NS // 2) % KE, at % (NS // 2)) if at < NCH * KE * NS // 2 else None

        def pair_no(c, m, i):
            return (c * KE + m) * (NS // 2) + i

        def da_bank(c, m, i, a):
            return (2 * pair_no(c, m, i) + a) % DA_BANKS

        def make_da(c, m, i):
            for a in range(2):
                b, rs = da_bank(c, m, i, a), pair_no(c, m, i) % RING
                if i == PE_PAIR:
                    dst, free = ring[:, rs, a, :], R.get(("ring_free", rs))
                else:
                    dst, free = psum_da[b][:, :], R.get(("da_free", b))
                S[c]["da", m, i, a] = act.put(lambda e, a=a, dst=dst: e.activation(
                    dst, dt[:, slot(c, m), :], ACT.Exp, scale=a_sb[:, m, 2 * i + a:2 * i + a + 1]),
                    (S[c]["dt", m], free, a_ready), k["c_da"])

        def make_u_pe(c, m):
            z = S[c]["wt_slot", m]
            for a in range(2):
                b = da_bank(c, m, PE_PAIR, a)
                for j in range(NJ):
                    t = pe.put(lambda e, a=a, b=b, j=j: e.matmul(
                        psum_da[b][:, j * P:(j + 1) * P], slots[:, z, j * P:(j + 1) * P],
                        bcb[:, 2 * PE_PAIR + a, 0, j * P:(j + 1) * P], start=True, stop=True),
                        (S[c]["wt", m], S[c]["diag"], R.get(("da_free", b))), k["c_u_pe"])
            R["u_pe"] = S[c]["u", m, PE_PAIR] = t
            free_slots.append((z, (t,)))

        def make_u(c, m, i):
            if i == PE_PAIR:
                free_slots.append((S[c]["ws", m], (R["u", i - 1], S[c]["w_transposed", m])))
                return
            rs = pair_no(c, m, i) % RING
            wb = slots[:, S[c]["ws", m], :].unsqueeze(1).broadcast_to([P, 2, TC])
            t = pool.put(lambda e: e.tensor_tensor(ring[:, rs, :, :], wb, bcb[:, 2 * i:2 * i + 2, 0, :], ALU.mult),
                         (S[c][f"w{m}"], S[c][f"piece{2 * i}"], S[c][f"piece{2 * i + 1}"], R.get(("ring_free", rs))),
                         k["c_u"])
            R[("u", i)] = S[c]["u", m, i] = t

        def scan_pair(c, m, i):
            n0, rs = 2 * i, pair_no(c, m, i) % RING
            tu = S[c]["u", m, i]
            on_dve = i in DVE_PAIRS[m]
            for a in range(2):
                n = n0 + a
                ta = S[c]["da", m, i, a]
                init = 0.0 if first(c) else state[:, m, n:n + 1]
                b = da_bank(c, m, i, a)
                in0, in1 = psum_da[b][:, :], ring[:, rs, a, :]
                if i == PE_PAIR:
                    in0, in1 = in1, in0
                dst = psum_da[b][:, :] if on_dve else ring[:, rs, a, :]
                ts = dve.put(lambda e, in0=in0, in1=in1, dst=dst, init=init: e.tensor_tensor_scan(
                    dst, in0, in1, init, ALU.mult, ALU.add),
                    (ta, tu, S[c].get(f"state{m}")),
                    k["c_scan"])
                R["da_free", b] = ts
                if on_dve:
                    dve.put(lambda e, n=n, b=b: e.tensor_copy(state[:, m, n:n + 1], psum_da[b][:, TC - 1:TC]), (ts,),
                            k["c_p_dve"])
                    tp = dve.put(lambda e, a=a, b=b, n=n: e.tensor_tensor(ring[:, rs, a, :], psum_da[b][:, :],
                                                                    bcb[:, n, 1, :], ALU.mult), (ts,), k["c_p_dve"])
                    R["state", m] = R["da_free", b] = tp
            if not on_dve:
                R["state", m] = tc = dve.put(lambda e: e.tensor_copy(state[:, m, n0:n0 + 2], ring[:, rs, :, TC - 1]),
                                             (ts,), k["c_p_dve"])
            nxt = after_pair(c, m, i, 1)
            if nxt:
                make_da(*nxt)
            nxt = after_pair(c, m, i, U_AHEAD)
            if nxt:
                make_u(*nxt)
            if not on_dve:
                tp = pool.put(lambda e: e.tensor_tensor(ring[:, rs, :, :], ring[:, rs, :, :], bcb[:, n0:n0 + 2, 1, :],
                                                        ALU.mult),
                              (tc, S[c][f"piece{n0}"], S[c][f"piece{n0 + 1}"]), k["c_p_pool"])
            R["p", i] = S[c]["p", m, i] = tp
            R["last of", i] = (c, m)

        def add_up(c, m, i):
            rs = pair_no(c, m, i) % RING
            if i == 0:
                for j in range(NJ):
                    t = pe.put(lambda e, j=j: e.matmul(psum_y[:, j * P:(j + 1) * P],
                                                       slots[:, S[c]["qs", m], j * P:(j + 1) * P],
                                                       ident[:, :], start=j == 0, stop=False, is_transpose=True,
                                                       skip_group_check=True),
                               (S[c][f"q{m}"], R.get("gate")), k["c_y"])
                free_slots.append((S[c]["qs", m], (t,)))
            for a in range(2):
                for j in range(NJ):
                    t = pe.put(lambda e, a=a, j=j: e.matmul(psum_y[:, j * P:(j + 1) * P],
                                                            ring[:, rs, a, j * P:(j + 1) * P], ident[:, :],
                                                            start=False, stop=i == NS // 2 - 1, is_transpose=True,
                                                            skip_group_check=True), (S[c]["p", m, i],), k["c_y"])
            R["ring_free", rs] = t
            S[c][f"y{m}"] = t

        def save_b_last(c):
            after = tuple(S[c][f"piece{n}"] for n in range(NS)) + (R.get("wq"),)
            n0 = 2 * PE_PAIR
            R["b_last"] = dve.put(lambda e: e.tensor_copy(b_last[:, 0:n0], bcb[:, 0:n0, 0, TC - 1]), after,
                                  k["c_blast"])
            for a in range(2):
                R["b_last_pe"] = sp.put(lambda e, a=a: e.dma_start(
                    b_last[:, n0 + a:n0 + a + 1], rows_dram[c][2 * (n0 + a), TC - 1:TC].partition_broadcast(P)),
                    (R.get("wq"),), k["c_blast_pe"], 16)

        def gate(c, m):
            R["gate"] = S[c][f"gate{m}"] = dve.put(
                lambda e: e.tensor_tensor(gated[:, :, :], psum_y[:, :].rearrange("p (j e) -> p j e", j=NJ),
                                          zs[:, :, m * P:(m + 1) * P], ALU.mult),
                (S[c][f"y{m}"], S[c]["zs"], R.get("gt")), k["c_gate"])

        def transpose_gated(c, m):
            b, fr = yield from take()
            for j in range(NJ):
                t = pe.put(lambda e, j=j, b=b: e.transpose(psum_f[b][:, j * P:(j + 1) * P], gated[:, j, :],
                                                          ident[:, :]), (S[c][f"gate{m}"], fr), k["c_gt"])
            R["gt"] = t
            yield 1
            t = act.put(lambda e: e.copy(yg[:, m, :], psum_f[b][:, :]), (t, R.get("outp")), k["c_gt_ev"])
            give(b, t)
            S[c]["yg"] = t

        def load_residual(c):
            S[c]["res"] = sp.put(lambda e: e.dma_start(x2[:, :, :], x[c * TC:(c + 1) * TC, :].rearrange(
                "(j p) d -> p j d", p=P)), (R.get("x2_free"),), k["c_xres"], 16)

        def project_out(c):
            S[c]["outp"] = []
            for h in range(NJ // 2):
                b, fr = yield from take()
                for j2 in range(2):
                    j = 2 * h + j2
                    for m in range(KE):
                        t = pe.put(lambda e, j=j, j2=j2, m=m, b=b: e.matmul(
                            psum_f[b][:, j2 * DM:(j2 + 1) * DM], yg[:, m, j * P:(j + 1) * P], w_out_sb[:, m, :],
                            start=m == 0, stop=m == KE - 1), (S[c]["yg"], fr, loaded_ffn), k["c_out"])
                    yield 1
                S[c]["outp"].append((b, t))
            R["outp"] = t

        def minus_mean_rstd(mv2, rstd2, nmr, after):
            d = dve.put(lambda e: e.tensor_tensor(nmr[:, :], mv2[:, :, 0], rstd2[:, :], ALU.mult), after,
                        k["c_rstd2"])
            return dve.put(lambda e: e.tensor_scalar(nmr[:, :], nmr[:, :], -1.0, None, ALU.mult), (d,), k["c_rstd2"])

        def attn_norm(c):
            stats2, mv2, rstd2, newton2, nmr = small["attn"]
            for j in range(NJ):
                b, t = S[c]["outp"][j // 2]
                d = dve.put(lambda e, j=j, b=b: e.bn_stats(stats2[:, j, :],
                                                          psum_f[b][:, (j % 2) * DM:(j % 2 + 1) * DM]), (t,),
                            k["c_stat2"])
            for j in range(NJ):
                d = dve.put(lambda e, j=j: e.bn_aggr(mv2[:, j, :], stats2[:, j, :]), (d,), k["c_stat2"])
            r = yield from rsqrt(mv2[:, :, 1], rstd2[:, :], (newton2[:, 0:NJ], newton2[:, NJ:]), ln_eps, 1.0,
                                    (d,), k["c_rstd2_a"], k["c_rstd2"])

            r = minus_mean_rstd(mv2, rstd2, nmr, (r,))
            yield 1
            for j in range(NJ):
                o = psum_f[S[c]["outp"][j // 2][0]][:, (j % 2) * DM:(j % 2 + 1) * DM]
                a = act.put(lambda e, j=j, o=o: e.activation(o, o, ACT.Identity, scale=rstd2[:, j:j + 1],
                                                             bias=nmr[:, j:j + 1]), (r,), k["c_on"])
            yield 1
            for h in range(NJ // 2):
                b = S[c]["outp"][h][0]
                d = dve.put(lambda e, h=h, b=b: e.tensor_tensor(
                    x2[:, 2 * h:2 * h + 2, :], x2[:, 2 * h:2 * h + 2, :],
                    psum_f[b][:, :].rearrange("p (j d) -> p j d", j=2), ALU.add), (a, S[c]["res"]), k["c_x2"])
                give(b, d)
            S[c]["x2"] = d

        def ffn_norm(c):
            stats2, mv2, rstd2, newton2, nmr = small["attn"]
            d = S[c]["x2"]
            for j in range(NJ):
                d = dve.put(lambda e, j=j: e.bn_stats(stats2[:, j, :], x2[:, j, :]), (S[c]["x2"],), k["c_stat2"])
            for j in range(NJ):
                d = dve.put(lambda e, j=j: e.bn_aggr(mv2[:, j, :], stats2[:, j, :]), (d,), k["c_stat2"])
            r = yield from rsqrt(mv2[:, :, 1], rstd2[:, :], (newton2[:, 0:NJ], newton2[:, NJ:]), ln_eps, 1.0,
                                    (d,), k["c_rstd2_a"], k["c_rstd2"])
            cd = k["c_rstd2"]
            d = dve.put(lambda e: e.tensor_copy(nmr[:, :], rstd2[:, :]), (r,), cd)
            d = dve.put(lambda e: e.tensor_tensor(mv2[:, :, 1], mv2[:, :, 1], rstd2[:, :], ALU.mult), (d,), cd)
            d = dve.put(lambda e: e.tensor_tensor(mv2[:, :, 1], mv2[:, :, 1], rstd2[:, :], ALU.mult), (d,), cd)
            r = yield from rsqrt(mv2[:, :, 1], rstd2[:, :], (newton2[:, 0:NJ], newton2[:, NJ:]), ln_eps, 1.0,
                                    (d,), k["c_rstd2_a"], k["c_rstd2"])
            r = dve.put(lambda e: e.tensor_tensor(rstd2[:, :], rstd2[:, :], nmr[:, :], ALU.mult), (r,), k["c_rstd2"])
            for j in range(NJ):
                d = dve.put(lambda e, j=j: e.tensor_scalar(stage[:, j, :], x2[:, j, :], mv2[:, j, 0:1],
                                                           rstd2[:, j:j + 1], ALU.subtract, ALU.mult),
                            (r,) + tuple(R["stage_free"]), k["c_h"])
            S[c]["h"] = d

        def transpose_h(c):
            S[c]["ht"] = []
            for i in range(KD):
                b, fr = yield from take()
                for j in range(NJ):
                    t = pe.put(lambda e, i=i, j=j, b=b: e.transpose(psum_f[b][:, j * P:(j + 1) * P],
                                                                   stage[:, j, i * P:(i + 1) * P], ident[:, :]),
                               (S[c]["h"], fr), k["c_ht"])
                S[c]["ht"].append((b, t))
                yield 1
            S[c]["stage_read"] = t
            for i, (b, t) in enumerate(S[c]["ht"]):
                t = act.put(lambda e, i=i, b=b: e.activation(h_t[:, i, :], psum_f[b][:, :], ACT.Identity,
                                                             scale=ln1_g_sb[:, i:i + 1], bias=ln1_b_sb[:, i:i + 1]),
                            (t, R.get("f1")), k["c_ht_ev"])
                give(b, t)
            S[c]["h_t"] = t

        def in_ring(c, half):
            return c == NCH - 1 and half == 1

        def ffn_up(c, half):
            hid = last_hidden if in_ring(c, half) else hidden
            hid_free = (R["ring_free", 0], R["ring_free", 1]) if in_ring(c, half) else (R.get("hid_free"),)
            for m in range(0, KH, 2):
                b, fr = yield from take()
                for m2 in range(2):
                    for i in range(KD):
                        t = pe.put(lambda e, i=i, m=m, m2=m2, b=b: e.matmul(
                            psum_f[b][:, m2 * HALF:(m2 + 1) * HALF], w1_sb[:, i, (m + m2) * P:(m + m2 + 1) * P],
                            h_t[:, i, half * HALF:(half + 1) * HALF], start=i == 0, stop=i == KD - 1),
                            (S[c]["h_t"], fr, R["ffn_ready"]), k["c_f1"])
                yield 2
                for m2 in range(2):
                    a = act.put(lambda e, m=m, m2=m2, b=b: e.activation(
                        hid[:, m + m2, :], psum_f[b][:, m2 * HALF:(m2 + 1) * HALF], ACT.Identity,
                        bias=b1_sb[:, m + m2:m + m2 + 1]),
                        (t,) + hid_free, k["c_up_ev"])
                give(b, a)
            R["f1"] = t
            for part in range(2):
                a2 = act.put(lambda e, part=part: e.activation(hid[:, 4 * part:4 * part + 4, :],
                                                               hid[:, 4 * part:4 * part + 4, :], ACT.Gelu), (a,),
                             k["c_gelu"])
            act.put(lambda e: e.preload_act_table_set(SCAN_TABLE))
            S[c][f"gelu{half}"] = a2

        def ffn_down(c, half):
            stats2, mv2, rstd2, newton2, nmr = small["hidden"]
            hid = last_hidden if in_ring(c, half) else hidden
            banks = []
            for _ in range(2):
                banks.append((yield from take()))
            for m in range(KH):
                for j in range(2):
                    b, fr = banks[j]
                    t = pe.put(lambda e, m=m, j=j, b=b: e.matmul(
                        psum_f[b][:, 0:DM + 1], hid[:, m, j * P:(j + 1) * P], w2_sb[:, m, :], start=m == 0,
                        stop=m == KH - 1, skip_group_check=True), (S[c][f"gelu{half}"], fr), k["c_f2"])
                if m % 2:
                    yield 1
            squared = []
            for part in range(2):
                h4 = hid[:, KH // 2 * part:KH // 2 * (part + 1), :]
                squared.append(act.put(lambda e, h4=h4: e.activation(h4, h4, ACT.Square), (t,), k["c_sq"]))
            yield 1
            for m in range(KH):
                for j in range(2):
                    b = banks[j][0]
                    t = pe.put(lambda e, m=m, j=j, b=b: e.matmul(
                        psum_f[b][:, DM + 1:DM + 2], hid[:, m, j * P:(j + 1) * P], w2_sb[:, m, DM:DM + 1],
                        start=False, stop=m == KH - 1, skip_group_check=True), (squared[m // (KH // 2)],), k["c_f2"])
            R["hid_free"] = t
            yield 2
            cd = k["c_ffn"]
            sl = slice(2 * half, 2 * half + 2)
            for j in range(2):
                b = banks[j][0]
                d = dve.put(lambda e, j=j, b=b: e.tensor_copy(mv2[:, 2 * half + j, :], psum_f[b][:, DM:DM + 2]),
                            (t,), cd)
            d = dve.put(lambda e: e.tensor_tensor(nmr[:, sl], mv2[:, sl, 0], mv2[:, sl, 0], ALU.mult), (d,), cd)
            d = dve.put(lambda e: e.tensor_tensor(mv2[:, sl, 1], mv2[:, sl, 1], nmr[:, sl], ALU.subtract), (d,), cd)
            d = dve.put(lambda e: e.tensor_scalar(mv2[:, sl, 1], mv2[:, sl, 1], 0.0, None, ALU.max), (d,), cd)
            r = yield from rsqrt(mv2[:, sl, 1], rstd2[:, sl], (newton2[:, sl],
                                                                           newton2[:, NJ + 2 * half:NJ + 2 * half + 2]),
                                 ln_eps, 1.0, (d,), k["c_rstd2_a"], k["c_rstd2"])
            for j in range(2):
                b, jj = banks[j][0], 2 * half + j
                d = dve.put(lambda e, b=b, jj=jj: e.scalar_tensor_tensor(
                    out=stage[:, jj, :], in0=psum_f[b][:, 0:DM], scalar=rstd2[:, jj:jj + 1], in1=bias_w2[:, :],
                    op0=ALU.mult, op1=ALU.add), (r, S[c]["stage_read"]), cd)
                give(b, d)
            S[c]["o"] = d

        def last_norm(c):
            stats2, mv2, rstd2, newton2, nmr = small["last"]
            for j in range(NJ):
                d = dve.put(lambda e, j=j: e.bn_stats(stats2[:, j, :], stage[:, j, :]), (S[c]["o"],), k["c_stat2"])
            for j in range(NJ):
                d = dve.put(lambda e, j=j: e.bn_aggr(mv2[:, j, :], stats2[:, j, :]), (d,), k["c_stat2"])
            r = yield from rsqrt(mv2[:, :, 1], rstd2[:, :], (newton2[:, 0:NJ], newton2[:, NJ:]), ln_eps, 1.0,
                                    (d,), k["c_rstd2_a"], k["c_rstd2"])
            r = minus_mean_rstd(mv2, rstd2, nmr, (r,))
            yield 1
            for j in range(NJ):
                a = act.put(lambda e, j=j: e.activation(stage[:, j, :], stage[:, j, :], ACT.Identity,
                                                        scale=rstd2[:, j:j + 1], bias=nmr[:, j:j + 1]), (r,), k["c_on"])
            yield 1
            d = dve.put(lambda e: e.tensor_tensor(x2[:, :, :], x2[:, :, :], stage[:, :, :], ALU.add), (a,),
                        k["c_res"])
            R["stage_free"] = [d]
            R["x2_free"] = sp.put(lambda e: e.dma_start(out[c * TC:(c + 1) * TC, :].rearrange(
                "(j p) d -> p j d", p=P), x2[:, :, :]), (d,), k["c_store"], 16)

        R = {}

        SIDE = [
            ("make_diagonals", 1, 0, make_diagonals, (("rope", 0),)),
            ("transpose_w0", 1, 0, lambda c: transpose_w(c, 0), (("make_wq0", 0),)),
            ("transpose_w1", 17, 0, lambda c: transpose_w(c, 1), (("make_wq1", 0),)),
            ("transpose_w2", 33, 0, lambda c: transpose_w(c, 2), (("make_wq2", 0),)),
            ("transpose_w3", 50, 0, lambda c: transpose_w(c, 3), (("make_wq3", 0),)),
            ("prepare_ffn", 3, 0, prepare_ffn, ()),
            ("make_wq1", 1, 0, lambda c: make_wq(c, 1), (("load_lam", 0), ("make_wq0", 0))),
            ("make_wq2", 16, 0, lambda c: make_wq(c, 2), (("make_wq1", 0),)),
            ("make_wq3", 42, 0, lambda c: make_wq(c, 3), (("make_wq2", 0),)),
            ("save_b_last", 41, 0, save_b_last, (("load_pieces", 0), ("make_wq3", 0))),
            ("project_z", 11, 0, project_z, (("transpose_x", 0), ("gate3", -1))),
            ("load_x", 14, 1, load_x, (("last_norm", -3), ("transpose_x", -1))),
            ("norm_x", 18, 1, norm_x, (("load_x", 0),)),
            ("transpose_x", 21, 1, transpose_x, (("norm_x", 0), ("project_z", -1))),
            ("project_x", 24, 1, project_x, (("transpose_x", 0),)),
            ("load_residual", 14, -1, load_residual, (("last_norm", -1),)),
            ("project_out", 17, -1, project_out, (("gated3", 0),)),
            ("attn_norm", 18, -1, attn_norm, (("project_out", 0), ("load_residual", 0))),
            ("ffn_norm", 25, -1, ffn_norm, (("attn_norm", 0), ("transpose_x", 2))),
            ("transpose_h", 29, -1, transpose_h, (("ffn_norm", 0), ("ffn_up1", -1))),
            ("project_dt", 29, 1, project_dt, (("project_x", 0),)),
            ("softplus_dt", 26, 1, softplus_dt, (("project_dt", 0),)),
            ("bc_norms", 32, 1, bc_norms, (("project_dt", 0),)),
            ("mean_dt", 42, 1, mean_dt, (("softplus_dt", 0),)),
            ("sums_dt", 43, 1, sums_dt, (("mean_dt", 0),)),
            ("angles", 44, 1, angles, (("sums_dt", 0),)),
            ("sines", 45, 1, sines, (("angles", 0),)),
            ("rope", 47, 1, rope, (("sines", 0), ("bc_norms", 0))),
            ("transpose_rows", 49, 1, transpose_rows, (("rope", 0),)),
            ("load_lam", 51, 1, load_lam, (("transpose_rows", 0), ("make_wq3", -1))),
            ("load_pieces", 53, 1, load_pieces, (("transpose_rows", 0), ("save_b_last", -1))),
            ("ffn_up0", 34, -1, lambda c: ffn_up(c, 0), (("transpose_h", 0), ("ffn_down1", -1))),
            ("ffn_down0", 43, -1, lambda c: ffn_down(c, 0), (("ffn_up0", 0), ("last_norm", -1))),
            ("ffn_up1", 53, -1, lambda c: ffn_up(c, 1), (("ffn_down0", 0),)),
            ("ffn_down1", 63, -1, lambda c: ffn_down(c, 1), (("ffn_up1", 0),)),
            ("last_norm", 7, -2, last_norm, (("ffn_down1", 0),)),
            ("make_wq0", 57, 1, lambda c: make_wq(c, 0), (("load_lam", 0), ("make_wq3", -1), ("save_b_last", -1))),
        ]
        finished = set()
        going = []

        def done(name, c):
            return (name, c) in finished or not 0 <= c < NCH

        def step(g_, now):
            if g_[0] > now or not all(done(n, g_[2] + d) for n, d in g_[4]):
                return
            g_[4] = ()
            if g_[1] is None:
                g_[1] = g_[5](g_[2])
            try:
                if g_[1] is not None:
                    g_[0] = now + next(g_[1])
                    return
            except StopIteration:
                pass
            finished.add((g_[3], g_[2]))
            going.remove(g_)

        def side(c, at):
            now = c * KE * NS + at
            for name, pos, which, stage_of, needs in SIDE:
                if name == "ffn_up1" and c + which == NCH - 1:
                    pos, needs = LAST_UP, (("ffn_up0", 0),)
                if pos == at and 0 <= c + which < NCH:
                    going.append([now, None, c + which, name, needs, stage_of])
            for g_ in list(going):
                step(g_, now)

        for at in range(KE * NS):
            side(-1, at)
        make_da(0, 0, 0)
        for i in range(U_AHEAD):
            make_u(0, 0, i)
        scanned = []
        for c in range(NCH + 2):
            for at in range(0, KE * NS, 2):
                m, i = at // NS, at % NS // 2
                if c < NCH:
                    scan_pair(c, m, i)
                    if i == PE_PAIR - 1:
                        make_u_pe(c, m)
                if i == GATE_AT and 0 < c * KE + m <= NCH * KE:
                    last = divmod(c * KE + m - 1, KE)
                    gate(*last)
                    finished.add((f"gate{last[1]}", last[0]))
                    going.append([c * KE * NS + at + 2, None, last[0], f"gated{last[1]}", (("project_out", -1),),
                                  lambda c_, m_=last[1]: transpose_gated(c_, m_)])
                side(c, at)
                side(c, at + 1)
                while scanned and not i < GATE_AT:
                    add_up(*scanned.pop(0))
                if i < GATE_AT and scanned and scanned[0][2] == NS // 2 - 1:
                    add_up(*scanned.pop(0))
                if c < NCH:
                    scanned.append((c, m, i))
        assert not going
        sp.put(lambda e: None, (R["x2_free"],))

        with nc.Block() as block:
            @block.sync
            def _(e):
                sp.run(e)

            @block.tensor
            def _(e):
                pe.run(e)

            @block.scalar
            def _(e):
                act.run(e)

            @block.vector
            def _(e):
                dve.run(e)

            @block.gpsimd
            def _(e):
                pool.run(e)


def kernel(**inputs):
    import concourse.bacc as bacc
    from concourse.bass_utils import run_bass_kernel_spmd

    a = {n.removeprefix("L0_"): np.asarray(v) for n, v in inputs.items()}
    x = a["attn_x"]
    B, L, DM = x.shape
    E, NS = a["attn_A_log"].shape
    HID = a["ffn_w1"].shape[0]

    def tiles(m):
        return np.ascontiguousarray(m.reshape(-1, P, m.shape[-1]).transpose(1, 0, 2))

    def columns(v):
        return np.ascontiguousarray(v.reshape(-1, P).T)

    order = np.concatenate([np.arange(2 * NS).reshape(2, NS).T.ravel(), [2 * NS, 2 * NS + 1]])
    arrays = {
        "x": x.reshape(B * L, DM),
        "w_in": tiles(a["attn_W_in"].T),
        "w_x": tiles(a["attn_W_x"].T[:, order]),
        "w_dt": columns(a["attn_W_dt"][:, 0]),
        "b_dt": columns(a["attn_b_dt"]),
        "a_log": tiles(a["attn_A_log"]),
        "bc_bias": np.stack([a["attn_B_bias"], a["attn_C_bias"]], 1),
        "bc_norm": np.stack([a["attn_B_norm_w"], a["attn_C_norm_w"]], 1),
        "freqs": a["attn_rope_freqs"],
        "d_skip": columns(a["attn_D"]),
        "w_out": tiles(a["attn_W_out"].T),
        "ln1_g": columns(a["ffn_ln1_g"]),
        "ln1_b": columns(a["ffn_ln1_b"]),
        "w1": tiles(a["ffn_w1"].T),
        "b1": columns(a["ffn_b1"]),
        "ln2_g": columns(a["ffn_ln2_g"]),
        "ln2_b": columns(a["ffn_ln2_b"]),
        "w2": tiles(a["ffn_w2"].T),
        "b2": a["ffn_b2"],
        "ident_in": np.eye(P, dtype=np.float32),
        "tri_in": np.triu(np.ones((P, P), np.float32)),
    }
    nc = bacc.Bacc("TRN2", target_bir_lowering=False, num_devices=1)
    arrays = {n: np.ascontiguousarray(v) for n, v in arrays.items()}
    args = {n: nc.dram_tensor(n, v.shape, mybir.dt.from_np(v.dtype), kind="ExternalInput").ap()
            for n, v in arrays.items()}
    out = nc.dram_tensor("out", (B * L, DM), F32, kind="ExternalOutput").ap()
    rows = nc.dram_tensor("rows", (B * L // TC, 2 * NS + 2, TC), F32, kind="Internal").ap()
    block_kernel(nc, out=out, rows_dram=rows, **args)
    r = run_bass_kernel_spmd(nc, [arrays], core_ids=[0])
    return r.results[0]["out"].reshape(B, L, DM)
```
